# Optimizing a Trainium2 kernel written in Bass

```python
import numpy as np
import jax
import jax.numpy as jnp

def _softmax(x, axis=-1):
    return jax.nn.softmax(x, axis=axis)

def _gelu(x):
    return jax.nn.gelu(x, approximate=True)

def _silu(x):
    return jax.nn.silu(x)

def _sigmoid(x):
    return jax.nn.sigmoid(x)

def _layernorm(x, axis=-1, eps=1e-05):
    m = jnp.mean(x, axis=axis, keepdims=True)
    v = jnp.var(x, axis=axis, keepdims=True)
    return (x - m) / jnp.sqrt(v + eps)

def _scatter_add(tgt, idx, src, axis=0):
    return tgt.at[idx].add(src)

def _segment_sum(src, seg, n):
    return jax.ops.segment_sum(src, seg, n)
kernel_name = 'mk_seq_preln_d2_jaxref_r8_01507e'

def setup_inputs(seed: int=0):
    np.random.seed(seed)
    _w = jnp.asarray

    def _L0_attn_setup():
        import jax, jax.numpy as jnp
        import numpy as np
        N_HEADS = 16
        D_HEAD = 128
        D_MODEL = 256
        MAXLEN = 256
        key = jax.random.key(seed)
        ks = jax.random.split(key, 9)
        b, t = (2, 256)
        hd = N_HEADS * D_HEAD
        init = 0.02
        return {'x': jax.random.normal(ks[0], (b, t, D_MODEL), dtype=jnp.float32), 'Wq': jax.random.normal(ks[1], (D_MODEL, hd), dtype=jnp.float32) * init, 'bq': jnp.zeros((hd,), dtype=jnp.float32), 'Wk': jax.random.normal(ks[2], (D_MODEL, hd), dtype=jnp.float32) * init, 'bk': jnp.zeros((hd,), dtype=jnp.float32), 'Wv': jax.random.normal(ks[3], (D_MODEL, hd), dtype=jnp.float32) * init, 'bv': jnp.zeros((hd,), dtype=jnp.float32), 'Wo': jax.random.normal(ks[4], (hd, D_MODEL), dtype=jnp.float32) * init, 'bo': jnp.zeros((D_MODEL,), dtype=jnp.float32)}
    _L0_attn_in = _L0_attn_setup()

    def _L0_ffn_setup():
        import jax, jax.numpy as jnp
        import numpy as np
        NUM_EXPERTS = 8
        TOP_K = 2
        key = jax.random.key(seed)
        k1, k2, k3, k4 = jax.random.split(key, 4)
        B, T, C, E, D = (4, 256, 256, NUM_EXPERTS, 256)
        scale = 0.02
        return {'x': jax.random.normal(k1, (B, T, C), dtype=jnp.float32), 'w_router': jax.random.normal(k2, (C, E), dtype=jnp.float32) * scale, 'w_fc': jax.random.normal(k3, (E, C, D), dtype=jnp.float32) * scale, 'w_proj': jax.random.normal(k4, (E, D, C), dtype=jnp.float32) * scale}
    _L0_ffn_in = _L0_ffn_setup()

    def _L1_attn_setup():
        import jax, jax.numpy as jnp
        import numpy as np
        HIDDEN = 256
        HEADS = 16
        HEAD_DIM = HIDDEN // HEADS
        NEG = -10000000000.0
        key = jax.random.key(seed)
        k1, k2, k3 = jax.random.split(key, 3)
        x = jax.random.normal(k1, (2, 256, HIDDEN), dtype=jnp.float32)
        w_qkv = jax.random.normal(k2, (HIDDEN, 3 * HIDDEN), dtype=jnp.float32) / np.sqrt(HIDDEN)
        w_out = jax.random.normal(k3, (HIDDEN, HIDDEN), dtype=jnp.float32) / np.sqrt(HIDDEN)
        return {'x': x, 'w_qkv': w_qkv, 'w_out': w_out}
    _L1_attn_in = _L1_attn_setup()

    def _L1_ffn_setup():
        import jax, jax.numpy as jnp
        import numpy as np
        E = 16
        TOP_K = 2
        key = jax.random.key(seed)
        k1, k2, k3, k4, k5 = jax.random.split(key, 5)
        H, I = (256, 176)
        scale = 0.02
        return {'hidden_states': jax.random.normal(k1, (4, 256, H), dtype=jnp.float32), 'gate_w': jax.random.normal(k2, (H, E), dtype=jnp.float32) * scale, 'w1': jax.random.normal(k3, (E, H, I), dtype=jnp.float32) * scale, 'w3': jax.random.normal(k4, (E, H, I), dtype=jnp.float32) * scale, 'w2': jax.random.normal(k5, (E, I, H), dtype=jnp.float32) * scale}
    _L1_ffn_in = _L1_ffn_setup()
    _d = {'L0_attn_x': _L0_attn_in['x'], 'L0_attn_Wq': _L0_attn_in['Wq'], 'L0_attn_bq': _L0_attn_in['bq'], 'L0_attn_Wk': _L0_attn_in['Wk'], 'L0_attn_bk': _L0_attn_in['bk'], 'L0_attn_Wv': _L0_attn_in['Wv'], 'L0_attn_bv': _L0_attn_in['bv'], 'L0_attn_Wo': _L0_attn_in['Wo'], 'L0_attn_bo': _L0_attn_in['bo'], 'L0_ffn_w_router': _L0_ffn_in['w_router'], 'L0_ffn_w_fc': _L0_ffn_in['w_fc'], 'L0_ffn_w_proj': _L0_ffn_in['w_proj'], 'L1_attn_w_qkv': _L1_attn_in['w_qkv'], 'L1_attn_w_out': _L1_attn_in['w_out'], 'L1_ffn_gate_w': _L1_ffn_in['gate_w'], 'L1_ffn_w1': _L1_ffn_in['w1'], 'L1_ffn_w3': _L1_ffn_in['w3'], 'L1_ffn_w2': _L1_ffn_in['w2']}
    _x0 = _d['L0_attn_x']
    _d['L0_attn_x'] = jax.random.normal(jax.random.fold_in(jax.random.key(seed), 1), (4, 512, 256), dtype=_x0.dtype)
    del _x0
    return _d

def reference(L0_attn_x, L0_attn_Wq, L0_attn_bq, L0_attn_Wk, L0_attn_bk, L0_attn_Wv, L0_attn_bv, L0_attn_Wo, L0_attn_bo, L0_ffn_w_router, L0_ffn_w_fc, L0_ffn_w_proj, L1_attn_w_qkv, L1_attn_w_out, L1_ffn_gate_w, L1_ffn_w1, L1_ffn_w3, L1_ffn_w2):

    def _L0_attn_ref(x, Wq, bq, Wk, bk, Wv, bv, Wo, bo):
        import jax, jax.numpy as jnp
        import numpy as np
        N_HEADS = 16
        D_HEAD = 128
        D_MODEL = 256
        MAXLEN = 256
        b, t, _ = x.shape
        h, dh = (N_HEADS, D_HEAD)
        scale = 1.0 / np.sqrt(dh).astype(np.float32)
        q = (x @ Wq + bq).reshape(b, h, t, dh)
        k = (x @ Wk + bk).reshape(b, t, h, dh).transpose(0, 2, 3, 1)
        v = (x @ Wv + bv).reshape(b, t, h, dh).transpose(0, 2, 1, 3)
        logits = jnp.einsum('bhtd,bhds->bhts', q, k) * scale
        mask = jnp.triu(jnp.full((t, t), -jnp.inf, dtype=x.dtype), k=1)
        weights = jax.nn.softmax(logits + mask, axis=-1)
        out = jnp.einsum('bhts,bhsd->bhtd', weights, v)
        out = out.transpose(0, 2, 1, 3).reshape(b, t, h * dh)
        return out @ Wo + bo

    def _L0_ffn_ref(x, w_router, w_fc, w_proj):
        import jax, jax.numpy as jnp
        import numpy as np
        NUM_EXPERTS = 8
        TOP_K = 2
        B, T, C = x.shape
        E = w_fc.shape[0]
        x_flat = x.reshape(-1, C)
        N = x_flat.shape[0]
        router_logits = x_flat @ w_router
        top_vals, top_idx = jax.lax.top_k(router_logits, TOP_K)
        probs = jax.nn.softmax(top_vals, axis=-1)
        rows = jnp.arange(N)[:, None]
        w_tok = jnp.zeros((N, E), dtype=x.dtype).at[rows, top_idx].add(probs)
        h = jnp.einsum('nc,ecd->ned', x_flat, w_fc)
        h = jnp.square(jax.nn.relu(h))
        y = jnp.einsum('ned,edc->nec', h, w_proj)
        out = jnp.einsum('nec,ne->nc', y, w_tok)
        return out.reshape(B, T, C)

    def _L1_attn_ref(x, w_qkv, w_out):
        import jax, jax.numpy as jnp
        import numpy as np
        HIDDEN = 256
        HEADS = 16
        HEAD_DIM = HIDDEN // HEADS
        NEG = -10000000000.0
        b, s, _ = x.shape
        qkv = x @ w_qkv
        qkv = qkv.reshape(b, s, 3, HEADS, HEAD_DIM)
        q, k, v = (qkv[:, :, 0], qkv[:, :, 1], qkv[:, :, 2])
        scale = jnp.sqrt(jnp.float32(HEAD_DIM)).astype(x.dtype)
        q = q / scale
        scores = jnp.einsum('bqhd,bkhd->bhqk', q, k)
        causal_mask = jnp.arange(s)[:, None] >= jnp.arange(s)[None, :]
        scores = jnp.where(causal_mask[None, None], scores, NEG)
        attn = jax.nn.softmax(scores, axis=-1)
        out = jnp.einsum('bhqk,bkhd->bqhd', attn, v).reshape(b, s, HIDDEN)
        return out @ w_out

    def _L1_ffn_ref(hidden_states, gate_w, w1, w3, w2):
        import jax, jax.numpy as jnp
        import numpy as np
        E = 16
        TOP_K = 2
        orig_shape = hidden_states.shape
        H = orig_shape[-1]
        x = hidden_states.reshape(-1, H)
        T = x.shape[0]
        router_logits = x @ gate_w
        probs = jax.nn.softmax(router_logits, axis=-1)
        topk_w, topk_i = jax.lax.top_k(probs, TOP_K)
        topk_w = topk_w / jnp.sum(topk_w, axis=-1, keepdims=True)
        combine = jnp.zeros((T, E), dtype=x.dtype)
        combine = combine.at[jnp.arange(T)[:, None], topk_i].add(topk_w)
        out = jnp.zeros_like(x)
        for e in range(E):
            gate_act = jax.nn.silu(x @ w1[e])
            up = x @ w3[e]
            y = gate_act * up @ w2[e]
            out = out + combine[:, e:e + 1] * y
        return out.reshape(orig_shape)
    x = L0_attn_x
    x = x + _L0_attn_ref(_layernorm(x, axis=-1), L0_attn_Wq, L0_attn_bq, L0_attn_Wk, L0_attn_bk, L0_attn_Wv, L0_attn_bv, L0_attn_Wo, L0_attn_bo)
    x = x + _L0_ffn_ref(_layernorm(x, axis=-1), L0_ffn_w_router, L0_ffn_w_fc, L0_ffn_w_proj)
    x = x + _L1_attn_ref(_layernorm(x, axis=-1), L1_attn_w_qkv, L1_attn_w_out)
    x = x + _L1_ffn_ref(_layernorm(x, axis=-1), L1_ffn_gate_w, L1_ffn_w1, L1_ffn_w3, L1_ffn_w2)
    return x

_drawn_inputs = setup_inputs


def setup_inputs(seed=0):
    import zlib

    import numpy as np

    out = dict(_drawn_inputs(seed))
    spreads = {'L0_attn_bq': (0.0, 0.8),
     'L0_attn_bk': (0.0, 0.8),
     'L0_attn_bv': (0.0, 0.1),
     'L0_attn_bo': (0.0, 0.1)}
    factors = {'L0_attn_Wq': 8.0,
     'L0_attn_Wk': 8.0,
     'L1_ffn_gate_w': 6.275,
     'L1_ffn_w1': 5.933,
     'L1_ffn_w3': 5.86,
     'L1_ffn_w2': 5.868}
    for name, (base, spread) in spreads.items():
        noise = np.random.default_rng([zlib.crc32(name.encode()), seed]).standard_normal(out[name].shape)
        drawn = base * np.exp(spread * noise) if base else spread * noise
        out[name] = jnp.asarray(drawn.astype(out[name].dtype))
    for name, factor in factors.items():
        out[name] = (out[name] * factor).astype(out[name].dtype)
    return out
```

```python
from contextlib import ExitStack

import numpy as np
import concourse.bass as bass
from concourse import mybir

F32 = mybir.dt.float32
F32R = mybir.dt.float32r
BF16 = mybir.dt.bfloat16
I32 = mybir.dt.int32
ALU = mybir.AluOpType
ACT = mybir.ActivationFunctionType
AX = mybir.AxisListType

P = 128
BATCH, SEQ, DM = 4, 512, 256
TOKENS = BATCH * SEQ
TILES = TOKENS // P
BT = SEQ // P
DK = DM // P
LN_EPS = 1e-5
MASKED = -1e30

TRI = [P * i * (i + 1) // 2 for i in range(BT)]
CAUSAL = P * BT * (BT + 1) // 2
KEY_AT = [sum((BT - j) * P for j in range(k)) for k in range(BT)]


def f32(ap):
    return ap.bitcast(F32)


def split_matmul(pe, out, stationary, moving, start, stop):
    (sh, sl), (mh, ml) = stationary, moving
    pe.matmul(out, sh, mh, start=start, stop=False)
    pe.matmul(out, sh, ml, start=False, stop=False)
    return pe.matmul(out, sl, mh, start=False, stop=stop)


class Memory:

    def __init__(self, nc, ctx, tag):
        self.nc, self.ctx, self.tag = nc, ctx, tag

    def sb(self, name, shape, dt=F32):
        return self.ctx.enter_context(self.nc.sbuf_tensor(f"{self.tag}_{name}", shape, dt))

    def pair(self, name, shape):
        return self.sb(name + "_hi", shape, F32R), self.sb(name + "_lo", shape, F32R)

    def ps(self, name, dt=F32, cols=512):
        return self.ctx.enter_context(self.nc.psum_tensor(f"{self.tag}_{name}", [P, cols], dt))

    def sem(self, name):
        return self.ctx.enter_context(self.nc.semaphore(f"{self.tag}_{name}"))


def both(pair, *index):
    return tuple(t[index] for t in pair)


def constants_phase(nc, x_dram, x_sb, ident, ident_bf, causal_bf):
    with ExitStack() as ctx:
        m = Memory(nc, ctx, "cst")
        x_loaded, zeroed, shaped = m.sem("x_loaded"), m.sem("zeroed"), m.sem("shaped")
        block = ctx.enter_context(nc.Block())

        @block.sync
        def _(sp):
            for b in range(BATCH):
                sp.dma_start(x_sb[:, b * BT:(b + 1) * BT, :],
                             x_dram[b].rearrange("(t p) d -> p t d", p=P)).then_inc(x_loaded, 16)
            sp.wait_ge(x_loaded, 16 * BATCH)

        @block.gpsimd
        def _(pool):
            pool.memset(ident[:, :], 0.0).then_inc(zeroed, 1)
            pool.memset(ident_bf[:, :], 0.0).then_inc(zeroed, 1)
            pool.memset(causal_bf[:, :], 0.0).then_inc(zeroed, 1)
            pool.wait_ge(zeroed, 3)
            for t in (ident, ident_bf):
                pool.affine_select(out=t[:, :], in_=t[:, :], compare_op=ALU.not_equal, fill=1.0,
                                   base=0, pattern=[[-1, P]], channel_multiplier=1).then_inc(shaped, 1)
            pool.affine_select(out=causal_bf[:, :], in_=causal_bf[:, :], compare_op=ALU.is_ge,
                               fill=MASKED, base=0, pattern=[[-1, P]],
                               channel_multiplier=1).then_inc(shaped, 1)
            pool.wait_ge(shaped, 3)


LN_SIGNALS = ("chain", "var_ready", "std_ready", "xn_ready", "turned_ready", "high_ready", "low_ready")


def layernorm_phase(nc, tag, signals, call, x_sb, ident, xnT, xn_all=None):
    with ExitStack() as ctx:
        m = Memory(nc, ctx, tag)
        stats = m.sb("stats", [P, TILES, 6])
        moments = m.sb("moments", [P, TILES, 2])
        std = m.sb("std", [P, TILES])
        rstd = m.sb("rstd", [P, TILES])
        if xn_all is None:
            places = 2
            xn = m.sb("xn", [P, places, BT, DM])
        else:
            places = BATCH
            xn = xn_all[:, :, :].rearrange("p (b t) d -> p b t d", b=BATCH)
        turned = [m.ps(f"turned{i}") for i in range(4)]
        chain, var_ready, std_ready, xn_ready, turned_ready, high_ready, low_ready = signals
        chained, batches, turns = call * (2 * TILES + 1), call * BATCH, call * DK * BATCH
        block = ctx.enter_context(nc.Block())

        @block.vector
        def _(dve):
            for t in range(TILES):
                dve.bn_stats(stats[:, t, :], x_sb[:, t, :]).then_inc(chain, 1)
            for t in range(TILES):
                dve.wait_ge(chain, chained + t + 1)
                dve.bn_aggr(moments[:, t, :], stats[:, t, :]).then_inc(chain, 1)
            dve.wait_ge(chain, chained + 2 * TILES)
            dve.tensor_scalar(std[:, :], moments[:, :, 1], LN_EPS, None, ALU.add).then_inc(var_ready, 1)
            dve.wait_ge(std_ready, call + 1)
            dve.reciprocal(rstd[:, :], std[:, :]).then_inc(chain, 1)
            dve.wait_ge(chain, chained + 2 * TILES + 1)

            def normalize(b):
                if b >= places:
                    dve.wait_ge(turned_ready, turns + DK * (b - places + 1))
                for t in range(BT):
                    i = b * BT + t
                    last = dve.tensor_scalar(xn[:, b % places, t, :], x_sb[:, i, :], moments[:, i, 0:1],
                                             rstd[:, i:i + 1], ALU.subtract, ALU.mult)
                last.then_inc(xn_ready, 1)

            normalize(0)
            for b in range(BATCH):
                if b + 1 < BATCH:
                    normalize(b + 1)
                for k in range(DK):
                    dve.wait_ge(high_ready, turns + DK * b + k + 1)
                    dve.tensor_tensor(xnT[1][:, k, b * SEQ:(b + 1) * SEQ], turned[(DK * b + k) % 4][:, :],
                                      f32(xnT[0][:, k, b * SEQ:(b + 1) * SEQ]),
                                      ALU.subtract).then_inc(low_ready, 1)

        @block.scalar
        def _(act):
            act.wait_ge(var_ready, call + 1)
            act.activation(std[:, :], std[:, :], ACT.Sqrt).then_inc(std_ready, 1)
            for n in range(DK * BATCH):
                b, k = divmod(n, DK)
                act.wait_ge(turned_ready, turns + n + 1)
                act.copy(xnT[0][:, k, b * SEQ:(b + 1) * SEQ], turned[n % 4][:, :]).then_inc(high_ready, 1)

        @block.tensor
        def _(pe):
            for n in range(DK * BATCH):
                b, k = divmod(n, DK)
                pe.wait_ge(xn_ready, batches + b + 1)
                if n >= 4:
                    pe.wait_ge(low_ready, turns + n - 3)
                for t in range(BT):
                    last = pe.transpose(turned[n % 4][:, t * P:(t + 1) * P],
                                        xn[:, b % places, t, k * P:(k + 1) * P], ident[:, :])
                last.then_inc(turned_ready, 1)


H0, DH0 = 16, 128
PAIRS = H0 // 2
UNITS = 2 * BATCH
CH = H0 * DH0 // P
QTOK = SEQ // CH
SCALE0 = float(np.float32(1.0) / np.sqrt(np.float32(DH0)))


def step_jobs(last):
    jobs = {}
    for slot in range(1, UNITS + 1):
        batch = (slot // 2 + 1) % BATCH
        if last and slot >= UNITS - 2:
            parts = [[], [], [], []]
        elif slot % 2 == 0:
            parts = [[], [("K", batch, 0)], [], [("K", batch, 1)]]
        elif slot < UNITS - 1:
            parts = [[], [("V", batch, 0)], [], [("V", batch, 1)]]
        else:
            q = [("Q", c, None) for c in range(CH // 2)]
            parts = [q[:2], q[2:5], q[5:], [("V", batch, 0), ("V", batch, 1)]]
        pair = (slot - 2) // 2
        parts.append([] if slot % 2 else [("O", pair, 0), ("O", pair, 1)])
        jobs[slot] = parts
    return jobs


JOBS = {last: step_jobs(last) for last in (False, True)}
PROLOGUE_JOBS = [("K", 0, 0), ("K", 0, 1), ("V", 0, 0), ("V", 0, 1)] + \
    [("Q", c, None) for c in range(CH // 2)] + [("K", 1, 0), ("K", 1, 1)]
STEP_JOBS = sum(len(part) for parts in JOBS[False].values() for part in parts)
STEP_SPLIT_JOBS = sum(len(part) for parts in JOBS[False].values() for part in parts[:4])


def job_numbers(last):
    n = s = 0
    numbered = {}
    for slot in range(1, UNITS + 1):
        for part in range(5):
            rows = []
            for job in JOBS[last][slot][part]:
                rows.append((job, n, s))
                n += 1
                s += job[0] != "O"
            numbered[slot, part] = rows
    return numbered


NUMBERED = {last: job_numbers(last) for last in (False, True)}


def index_of(kind, *where):
    return next(n for rows in NUMBERED[False].values() for job, n, _ in rows if job == (kind, *where))


def attention0_phase(nc, x_sb, xnT, ident, ident_bf, causal_bf, Wq, bq, Wk, bk, Wv, bv, Wo, bo):
    with ExitStack() as ctx:
        m = Memory(nc, ctx, "a0")
        wq = m.pair("wq", [P, DK, H0 * DH0])
        wk = m.pair("wk", [P, DK, 2 * DH0])
        wv = m.pair("wv", [P, DK, 2 * DH0])
        wo = m.pair("wo", [P, 2, DM])
        w_raw = m.sb("w_raw", [P, 3, 2, 2 * DH0])
        bias_rows = m.sb("bias_rows", [3 * H0, P])
        bias_all = m.sb("bias_all", [P, 3, H0])
        bias_pair = m.sb("bias_pair", [P, 2, 2])
        bo_all = m.sb("bo_all", [P, DM])
        qT = m.pair("qT", [P, BATCH * 2 * SEQ])
        kT = [m.pair(f"kT{i}", [P, 2 * SEQ]) for i in range(2)]
        vv = [m.pair(f"v{i}", [P, BT * 2 * DH0]) for i in range(2)]
        probs = [m.sb(f"probs{i}", [P, CAUSAL]) for i in range(2)]
        pT = m.pair("pT", [P, CAUSAL])
        oT = m.pair("oT", [P, 2, SEQ])
        ones = m.sb("ones", [P, 1])
        peak = m.sb("peak", [P, 2, BT])
        shift = m.sb("shift", [P, 2, BT])
        total = m.sb("total", [P, 2, BT])
        inverse = m.sb("inverse", [P, 2, BT])

        score_bank = [m.ps(f"score{i}") for i in range(3)]
        turn_bank = [m.ps(f"turn{i}") for i in range(2)]
        out_bank = m.ps("out")
        proj_bank = [m.ps(f"proj{i}") for i in range(2)]

        wq_loaded = [m.sem(f"wq_loaded{k}") for k in range(DK)]
        wq_high, wq_split = m.sem("wq_high"), m.sem("wq_split")
        bias_loaded, bias_done, weights_loaded = m.sem("bias_loaded"), m.sem("bias_done"), m.sem("weights_loaded")
        ones_ready = m.sem("ones_ready")
        raw_high, bias_turned = m.sem("raw_high"), m.sem("bias_turned")
        wk_split, wv_split, wo_split = m.sem("wk_split"), m.sem("wv_split"), m.sem("wo_split")
        bk_staged, bv_staged = m.sem("bk_staged"), m.sem("bv_staged")
        proj_ready, proj_high, proj_read = m.sem("proj_ready"), m.sem("proj_high"), m.sem("proj_read")
        scores_ready, peaks, shift_ready = m.sem("scores_ready"), m.sem("peaks"), m.sem("shift_ready")
        exp_done, inverse_ready, probs_ready = m.sem("exp_done"), m.sem("inverse_ready"), m.sem("probs_ready")
        turn_ready, turn_high, turn_read = m.sem("turn_ready"), m.sem("turn_high"), m.sem("turn_read")
        out_ready, out_high, out_read = m.sem("out_ready"), m.sem("out_high"), m.sem("out_read")

        SCORE_TILES = [[(0, 0), (2, P)], [(1, 0)], [(3, 0)]]
        STAT = {0: 0, 2: 1, 1: 2, 3: 3}
        STATS_OF_BANK = [(0, 2), (2, 3), (3, 4)]
        TURN_TILES = [[0], [1], [2, 3]]

        block = ctx.enter_context(nc.Block())

        def job_at(p, n):
            return len(PROLOGUE_JOBS) + STEP_JOBS * p + n

        def split_at(p, n):
            return len(PROLOGUE_JOBS) + STEP_SPLIT_JOBS * p + n

        def bank_of(n):
            return proj_bank[n % 2]

        assert len(PROLOGUE_JOBS) % 2 == 0 and STEP_JOBS % 2 == 0

        @block.sync
        def _(sp):
            for i, b in enumerate((bq, bk, bv)):
                sp.dma_start(bias_rows[i * H0:(i + 1) * H0, :], b.rearrange("(h p) -> h p", p=P)).then_inc(bias_loaded, 16)
            sp.dma_start(bo_all[:, :], bo.rearrange("(a d) -> a d", a=1).to_broadcast([P, DM])).then_inc(bias_loaded, 16)
            for c in range(BATCH):
                for k in range(DK):
                    if c >= 1:
                        sp.wait_ge(wq_split, DK * (c - 1) + k + 1)
                    sp.dma_start(probs[k][:, 0:SEQ], Wq[k * P:(k + 1) * P, c * SEQ:(c + 1) * SEQ]).then_inc(wq_loaded[k], 16)

            def load_pair(p):
                for i, w in enumerate((Wk, Wv)):
                    sp.dma_start(w_raw[:, i, :, :], w.rearrange("(k p) n -> p k n", p=P)[:, :, bass.ds(p * 2 * DH0, 2 * DH0)]).then_inc(weights_loaded, 16)
                sp.dma_start(w_raw[:, 2, :, :], Wo.rearrange("(h p) n -> p h n", p=P)[:, bass.ds(p * 2, 2), :]).then_inc(weights_loaded, 16)

            load_pair(0)
            with sp.Fori(1, PAIRS) as p:
                sp.wait_ge(wo_split, p)
                load_pair(p)

        @block.gpsimd
        def _(pool):
            def split_weights(i, pair, count, done):
                raw = w_raw[:, i, :, :].rearrange("p a n -> p (a n)")
                pool.tensor_tensor(pair[0][:, :, :].rearrange("p a n -> p (a n)"), raw, ones[:, 0:1].to_broadcast([P, 4 * DH0]),
                                   ALU.mult).then_inc(raw_high, 1)
                pool.wait_ge(raw_high, count + 1)
                pool.tensor_tensor(pair[1][:, :, :], w_raw[:, i, :, :], f32(pair[0][:, :, :]), ALU.subtract).then_inc(done, 1)

            def normalize(p, u):
                pool.wait_ge(inverse_ready, UNITS * p + u + 1)
                for i in range(BT):
                    rows = probs[u % 2][:, TRI[i]:TRI[i] + (i + 1) * P]
                    by = inverse[:, u % 2, STAT[i]:STAT[i] + 1]
                    if i == 0:
                        last = pool.tensor_tensor(rows, rows, by.to_broadcast([P, P]), ALU.mult)
                    else:
                        last = pool.tensor_scalar(rows, rows, by, 1.0, ALU.mult, ALU.mult)
                last.then_inc(probs_ready, 1)

            def step(p, last):
                if not isinstance(p, int) or p > 0:
                    pool.wait_ge(proj_ready, job_at(p, 0))
                split_weights(2, wo, 3 * p + 2, wo_split)
                for u in range(1, UNITS + 1):
                    if u == UNITS and last:
                        break
                    normalize(p, u)
                    if last:
                        continue
                    if u == 4:
                        pool.wait_ge(weights_loaded, 16 * 3 * (p + 2))
                        pool.wait_ge(proj_ready, job_at(p, index_of("K", 3, 1)) + 1)
                        split_weights(0, wk, 3 * p + 3, wk_split)
                    if u == 5:
                        pool.wait_ge(proj_ready, job_at(p, index_of("V", 3, 1)) + 1)
                        split_weights(1, wv, 3 * p + 4, wv_split)

            pool.memset(ones[:, :], 1.0).then_inc(ones_ready, 1)
            pool.wait_ge(ones_ready, 1)
            pool.wait_ge(weights_loaded, 16 * 3)
            split_weights(0, wk, 0, wk_split)
            split_weights(1, wv, 1, wv_split)
            normalize(0, 0)
            step(0, False)
            with pool.Fori(1, PAIRS - 1) as p:
                step(p, False)
            step(PAIRS - 1, True)

        @block.tensor
        def _(pe):
            def project(job, p, n, p_of_data):
                kind, a, b = job
                bank = bank_of(n)
                if kind == "K":
                    for k in range(DK):
                        last = split_matmul(pe, bank[:, :], both(wk, slice(None), k, slice(b * DH0, (b + 1) * DH0)),
                                            both(xnT, slice(None), k, slice(a * SEQ, (a + 1) * SEQ)), k == 0, k == DK - 1)
                elif kind == "V":
                    for t in (2 * b, 2 * b + 1):
                        at = a * SEQ + t * P
                        for k in range(DK):
                            last = split_matmul(pe, bank[:, t % 2 * 256:t % 2 * 256 + 256],
                                                both(xnT, slice(None), k, slice(at, at + P)),
                                                both(wv, slice(None), k), k == 0, k == DK - 1)
                elif kind == "Q":
                    for c in (2 * a, 2 * a + 1):
                        for k in range(DK):
                            tokens = tuple(x[:, k, :].rearrange("p (b t) -> p b t", b=BATCH)[:, :, bass.ds(p_of_data * 2 * QTOK, 2 * QTOK)] for x in xnT)
                            out = bank[:, c % 2 * 256:c % 2 * 256 + 256].rearrange("p (b t) -> p b t", b=BATCH)
                            last = split_matmul(pe, out, both(wq, slice(None), k, slice(c * P, (c + 1) * P)),
                                                tokens, k == 0, k == DK - 1)
                else:
                    for t in (2 * b, 2 * b + 1):
                        for j in range(2):
                            last = split_matmul(pe, bank[:, t % 2 * 256:t % 2 * 256 + 256],
                                                both(oT, slice(None), j, slice(t * P, (t + 1) * P)),
                                                both(wo, slice(None), j), j == 0, j == 1)
                last.then_inc(proj_ready, 1)

            def jobs(p, slot, part, last):
                for job, n, _ in NUMBERED[last][slot, part]:
                    pe.wait_ge(proj_read, job_at(p, n) - 1)
                    project(job, p, n, p + 1)

            def scores(u, bank):
                b, j = divmod(u % UNITS, 2)
                for i, col in SCORE_TILES[bank]:
                    out = score_bank[bank][:, col:col + (i + 1) * P]
                    queries = both(qT, slice(None), slice((2 * b + j) * SEQ + i * P, (2 * b + j) * SEQ + (i + 1) * P))
                    split_matmul(pe, out, queries, both(kT[b % 2], slice(None), slice(j * SEQ, j * SEQ + (i + 1) * P)), True, False)
                    last = pe.matmul(out[:, i * P:], ident_bf[:, :], causal_bf[:, :], start=False, stop=True)
                last.then_inc(scores_ready, 1)

            def turn(u, group):
                col = 0
                for k in TURN_TILES[group]:
                    for i in range(k, BT):
                        last = pe.transpose(turn_bank[group % 2][:, col:col + P],
                                            probs[u % 2][:, TRI[i] + k * P:TRI[i] + (k + 1) * P], ident[:, :])
                        col += P
                last.then_inc(turn_ready, 1)

            def weigh(u, k):
                b, j = divmod(u, 2)
                at = k * 2 * DH0 + j * DH0
                return split_matmul(pe, out_bank[:, k * P:], both(vv[b % 2], slice(None), slice(at, at + DH0)),
                                    both(pT, slice(None), slice(KEY_AT[k], KEY_AT[k] + (BT - k) * P)), k == 0, k == BT - 1)

            def slot(p, u, last=False):
                g = UNITS * p + u
                score = not (last and u == UNITS)
                pe.wait_ge(probs_ready, g)
                pe.wait_ge(turn_read, 3 * g - 3)
                turn(u - 1, 0)
                if score:
                    pe.wait_ge(exp_done, 3 * g - 2)
                    if u == 2:
                        pe.wait_ge(proj_read, job_at(p, 0))
                    elif u % 2 == 0:
                        made = index_of("Q", CH // 2 - 1, None) if u == UNITS else index_of("K", u // 2, 1)
                        pe.wait_ge(proj_read, job_at(p, made) + 1)
                    scores(u, 0)
                turn(u - 1, 1)
                if score:
                    pe.wait_ge(exp_done, 3 * g - 1)
                    scores(u, 1)
                    pe.wait_ge(exp_done, 3 * g)
                    scores(u, 2)
                pe.wait_ge(turn_read, 3 * g - 2)
                pe.wait_ge(out_read, g - 1)
                if u % 2 and u > 1:
                    pe.wait_ge(proj_read, job_at(p, index_of("V", u // 2, 1)) + 1)
                weigh(u - 1, 0)
                turn(u - 1, 2)
                jobs(p, u, 0, last)
                pe.wait_ge(turn_read, 3 * g - 1)
                weigh(u - 1, 1)
                jobs(p, u, 1, last)
                pe.wait_ge(turn_read, 3 * g)
                weigh(u - 1, 2)
                jobs(p, u, 2, last)
                weigh(u - 1, 3).then_inc(out_ready, 1)
                jobs(p, u, 3, last)
                if u % 2 == 0:
                    pe.wait_ge(out_read, g)
                    jobs(p, u, 4, last)

            def step(p, last=False):
                for u in range(1, UNITS + 1):
                    if u == 2:
                        pe.wait_ge(wo_split, p + 1)
                    if u == UNITS - 2 and not last:
                        pe.wait_ge(wk_split, p + 2)
                    if u == UNITS - 1 and not last:
                        pe.wait_ge(wv_split, p + 2)
                    slot(p, u, last)

            pe.wait_ge(bias_loaded, 16 * 4)
            pe.transpose(turn_bank[0][:, 0:3 * H0], bias_rows[:, :], ident[0:3 * H0, 0:3 * H0]).then_inc(bias_turned, 1)
            pe.wait_ge(wk_split, 1)
            for n, job in enumerate(PROLOGUE_JOBS):
                if job[0] == "V":
                    pe.wait_ge(wv_split, 1)
                if job[0] == "Q":
                    pe.wait_ge(wq_split, DK * (2 * job[1] * P // SEQ + 1))
                if n >= 2:
                    pe.wait_ge(proj_read, n - 1)
                project(job, 0, n, 0)
                if n == len(PROLOGUE_JOBS) - 3:
                    pe.wait_ge(proj_read, n + 1)
                    for bank in range(3):
                        scores(0, bank)
            step(0)
            with pe.Fori(1, PAIRS - 1) as p:
                step(p)
            step(PAIRS - 1, True)

        def evacuation(job, n):
            kind, a, b = job
            bank = bank_of(n)
            if kind == "K":
                return [(both(kT[a % 2], slice(None), slice(b * SEQ, (b + 1) * SEQ)), bank[:, :], bias_pair[:, 0, b:b + 1])]
            if kind == "V":
                return [(both(vv[a % 2], slice(None), slice(b * 512, (b + 1) * 512)), bank[:, :], None)]
            pieces = []
            for c in (2 * a, 2 * a + 1):
                out = tuple(x[:, :].rearrange("p (t c) -> p t c", c=CH)[:, :, c] for x in qT)
                pieces.append((out, bank[:, c % 2 * 256:c % 2 * 256 + 256], bias_all[:, 0, c:c + 1]))
            return pieces

        @block.scalar
        def _(act):
            def high(p, job, n, s):
                act.wait_ge(proj_ready, n_of(p, n) + 1)
                for out, src, bias in evacuation(job, n):
                    last = act.copy(out[0], src) if bias is None else act.activation(out[0], src, ACT.Identity, bias=bias)
                last.then_inc(proj_high, 1)

            def n_of(p, n):
                return n if p is None else job_at(p, n)

            def jobs(p, slot, part, last):
                for job, n, s in NUMBERED[last][slot, part]:
                    high(p, job, n, s)

            def exps(p, u, bank):
                g = UNITS * p + u
                act.wait_ge(shift_ready, 3 * g + bank + 1)
                for i, col in SCORE_TILES[bank]:
                    c = STAT[i]
                    last = act.activation(probs[u % 2][:, TRI[i]:TRI[i] + (i + 1) * P], score_bank[bank][:, col:col + (i + 1) * P],
                                          ACT.Exp, bias=shift[:, u % 2, c:c + 1], scale=SCALE0, accum_out=total[:, u % 2, c:c + 1])
                last.then_inc(exp_done, 1)

            def turned(p, u, group):
                g = UNITS * p + u
                act.wait_ge(turn_ready, 3 * g - 2 + group)
                at = KEY_AT[TURN_TILES[group][0]]
                width = sum((BT - k) * P for k in TURN_TILES[group])
                act.copy(pT[0][:, at:at + width], turn_bank[group % 2][:, 0:width]).then_inc(turn_high, 1)

            def slot(p, u, last=False):
                g = UNITS * p + u
                score = not (last and u == UNITS)
                turned(p, u, 0)
                turned(p, u, 1)
                if score:
                    exps(p, u, 0)
                    exps(p, u, 1)
                turned(p, u, 2)
                if score:
                    exps(p, u, 2)
                for part in range(3):
                    jobs(p, u, part, last)
                act.wait_ge(out_ready, g)
                j = (u - 1) % 2
                act.activation(oT[0][:, j, :], out_bank[:, :], ACT.Identity, bias=bias_pair[:, 1, j:j + 1]).then_inc(out_high, 1)
                jobs(p, u, 3, last)

            def step(p, last=False):
                for u in range(1, UNITS + 1):
                    if u == 1:
                        act.wait_ge(bv_staged, p + 1)
                    if u == UNITS - 2 and not last:
                        act.wait_ge(bk_staged, p + 2)
                    slot(p, u, last)

            for c in range(BATCH):
                for k in range(DK):
                    act.wait_ge(wq_loaded[k], 16 * (c + 1))
                    act.copy(wq[0][:, k, c * SEQ:(c + 1) * SEQ], probs[k][:, 0:SEQ]).then_inc(wq_high, 1)
            act.wait_ge(bk_staged, 1)
            for n, job in enumerate(PROLOGUE_JOBS):
                high(None, job, n, n)
                if n == len(PROLOGUE_JOBS) - 3:
                    for bank in range(3):
                        exps(0, 0, bank)
            step(0)
            with act.Fori(1, PAIRS - 1) as p:
                step(p)
            step(PAIRS - 1, True)

        @block.vector
        def _(dve):
            def low(p, job, n, s):
                dve.wait_ge(proj_high, (s if p is None else split_at(p, s)) + 1)
                for out, src, bias in evacuation(job, n):
                    if bias is None:
                        last = dve.tensor_tensor(out[1], src, f32(out[0]), ALU.subtract)
                    else:
                        last = dve.scalar_tensor_tensor(out[1], src, bias, f32(out[0]), ALU.add, ALU.subtract)
                last.then_inc(proj_read, 1)

            def jobs(p, slot, part, last):
                for job, n, s in NUMBERED[last][slot, part]:
                    if job[0] != "O":
                        low(p, job, n, s)
                        continue
                    _, b, half = job
                    dve.wait_ge(proj_ready, job_at(p, n) + 1)
                    t = b * BT + 2 * half
                    rows = x_sb[:, t:t + 2, :].rearrange("p t d -> p (t d)")
                    dve.tensor_tensor(rows, bank_of(n)[:, :], rows, ALU.add).then_inc(proj_read, 1)

            def peak_of(p, u, bank):
                g = UNITS * p + u
                dve.wait_ge(scores_ready, 3 * g + bank + 1)
                for i, col in SCORE_TILES[bank]:
                    c = STAT[i]
                    last = dve.reduce_max(peak[:, u % 2, c:c + 1], score_bank[bank][:, col:col + (i + 1) * P], AX.X)
                last.then_inc(peaks, 1)
                dve.wait_ge(peaks, 3 * g + bank + 1)
                lo, hi = STATS_OF_BANK[bank]
                dve.tensor_scalar(shift[:, u % 2, lo:hi], peak[:, u % 2, lo:hi], -SCALE0, None, ALU.mult).then_inc(shift_ready, 1)

            def invert(p, u):
                g = UNITS * p + u
                dve.wait_ge(exp_done, 3 * g + 3)
                dve.reciprocal(inverse[:, u % 2, :], total[:, u % 2, :]).then_inc(inverse_ready, 1)

            def turned(p, u, group):
                g = UNITS * p + u
                dve.wait_ge(turn_high, 3 * g - 2 + group)
                at = KEY_AT[TURN_TILES[group][0]]
                width = sum((BT - k) * P for k in TURN_TILES[group])
                dve.tensor_tensor(pT[1][:, at:at + width], turn_bank[group % 2][:, 0:width],
                                  f32(pT[0][:, at:at + width]), ALU.subtract).then_inc(turn_read, 1)

            def slot(p, u, last=False):
                g = UNITS * p + u
                score = not (last and u == UNITS)
                turned(p, u, 0)
                if score:
                    peak_of(p, u, 0)
                turned(p, u, 1)
                if score:
                    peak_of(p, u, 1)
                    peak_of(p, u, 2)
                turned(p, u, 2)
                if score:
                    invert(p, u)
                for part in range(3):
                    jobs(p, u, part, last)
                dve.wait_ge(out_high, g)
                j = (u - 1) % 2
                dve.scalar_tensor_tensor(oT[1][:, j, :], out_bank[:, :], bias_pair[:, 1, j:j + 1], f32(oT[0][:, j, :]),
                                         ALU.add, ALU.subtract).then_inc(out_read, 1)
                jobs(p, u, 3, last)
                jobs(p, u, 4, last)

            def step(p, last=False):
                dve.tensor_copy(bias_pair[:, 1, :], bias_all[:, 2, bass.ds(p * 2, 2)]).then_inc(bv_staged, 1)
                dve.wait_ge(bv_staged, p + 1)
                for u in range(1, UNITS + 1):
                    if u == UNITS - 2 and not last:
                        dve.tensor_copy(bias_pair[:, 0, :], bias_all[:, 1, bass.ds(p * 2 + 2, 2)]).then_inc(bk_staged, 1)
                        dve.wait_ge(bk_staged, p + 2)
                    slot(p, u, last)

            dve.wait_ge(bias_turned, 1)
            dve.tensor_copy(bias_all[:, :, :], turn_bank[0][:, 0:3 * H0]).then_inc(bias_done, 1)
            dve.wait_ge(bias_done, 1)
            dve.tensor_copy(bias_pair[:, 0, :], bias_all[:, 1, 0:2]).then_inc(bk_staged, 1)
            for t in range(TILES):
                dve.tensor_tensor(x_sb[:, t, :], x_sb[:, t, :], bo_all[:, :], ALU.add).then_inc(bias_done, 1)
            for c in range(BATCH):
                for k in range(DK):
                    dve.wait_ge(wq_high, DK * c + k + 1)
                    cols = slice(c * SEQ, (c + 1) * SEQ)
                    dve.tensor_tensor(wq[1][:, k, cols], probs[k][:, 0:SEQ], f32(wq[0][:, k, cols]), ALU.subtract).then_inc(wq_split, 1)
            dve.wait_ge(bias_done, 1 + TILES)
            dve.wait_ge(bk_staged, 1)
            for n, job in enumerate(PROLOGUE_JOBS):
                low(None, job, n, n)
                if n == len(PROLOGUE_JOBS) - 3:
                    for bank in range(3):
                        peak_of(0, 0, bank)
                    invert(0, 0)
            step(0)
            with dve.Fori(1, PAIRS - 1) as p:
                step(p)
            step(PAIRS - 1, True)

E0, DF0 = 8, 256
FK0 = DF0 // P
CHUNKS = BATCH


def moe0_phase(nc, x_sb, xnT, w_router, w_fc, w_proj):
    with ExitStack() as ctx:
        m = Memory(nc, ctx, "m0")
        router_raw = m.sb("router_raw", [P, DK, E0])
        router = m.pair("router", [P, DK, E0])
        logits = m.sb("logits", [P, TILES, E0])
        top = m.sb("top", [P, TILES, 8])
        top_at = m.sb("top_at", [P, TILES, 8], mybir.dt.uint32)
        top_id = m.sb("top_id", [P, TILES, 8])
        expert_id = m.sb("expert_id", [P, E0])
        gap = m.sb("gap", [P, TILES])
        share = m.sb("share", [P, 2, TILES])
        hit = m.sb("hit", [P, 2, TILES * E0])
        combine = m.sb("combine", [P, TILES, E0])
        ones = m.sb("ones", [P, 1])
        w_raw = [m.sb(f"w_raw{i}", [P, 2, 2 * DM]) for i in range(2)]
        fc = [m.pair(f"fc{i}", [P, DK, DF0]) for i in range(2)]
        proj = [m.pair(f"proj{i}", [P, FK0, DM]) for i in range(2)]
        relu = m.sb("relu", [P, 2, SEQ])
        square = m.sb("square", [P, 2, SEQ])
        hT = [m.pair(f"hT{i}", [P, FK0, SEQ]) for i in range(2)]
        up_bank = [m.ps(f"up{i}") for i in range(4)]
        down_bank = [m.ps(f"down{i}") for i in range(4)]

        router_loaded, router_high, router_split = m.sem("router_loaded"), m.sem("router_high"), m.sem("router_split")
        logits_ready, chain, ids_ready, gap_ready, exp_ready = (m.sem(n) for n in ("logits_ready", "chain", "ids_ready", "gap_ready", "exp_ready"))
        combine_ready = m.sem("combine_ready")
        raw_loaded = [m.sem(f"raw_loaded{i}") for i in range(2)]
        raw_high = m.sem("raw_high")
        split_done = [m.sem(f"split_done{i}") for i in range(2)]
        up_ready, relu_ready, square_ready, high_ready, low_ready = (m.sem(n) for n in ("up_ready", "relu_ready", "square_ready", "high_ready", "low_ready"))
        down_ready, down_read = m.sem("down_ready"), m.sem("down_read")
        block = ctx.enter_context(nc.Block())
        STEPS = E0 // 2
        PER_STEP = 2 * CHUNKS

        def fc_of(e):
            return w_fc[e].rearrange("(k p) n -> p k n", p=P)

        @block.sync
        def _(sp):
            sp.dma_start(router_raw[:, :, :], w_router.rearrange("(k p) e -> p k e", p=P)).then_inc(router_loaded, 16)

            def load(e, i, done):
                if not isinstance(done, int) or done > 0:
                    sp.wait_ge(split_done[i], done)
                for j, w in enumerate((w_fc, w_proj)):
                    src = w.rearrange("e (k p) n -> p e k n", p=P)[:, bass.ds(e, 1), :, :]
                    sp.dma_start(w_raw[i][:, j, :].rearrange("p (a k n) -> p a k n", a=1, k=DK), src).then_inc(raw_loaded[i], 16)

            load(0, 0, 0)
            load(1, 1, 0)
            with sp.Fori(1, STEPS) as p:
                load(2 * p, 0, p)
                load(2 * p + 1, 1, p)

        @block.gpsimd
        def _(pool):
            pool.memset(ones[:, :], 1.0).then_inc(raw_high, 1)
            pool.iota(expert_id[:, :], pattern=[[1, E0]], base=0, channel_multiplier=0,
                      allow_small_or_imprecise_dtypes=True).then_inc(ids_ready, 1)
            pool.wait_ge(raw_high, 1)

            def split_weights(i, p, count):
                pool.wait_ge(raw_loaded[i], 32 * (p + 1))
                for j, pair in enumerate((fc[i], proj[i])):
                    raw = w_raw[i][:, j, :]
                    high, low = (t[:, :, :].rearrange("p k n -> p (k n)") for t in pair)
                    pool.tensor_tensor(high, raw, ones[:, 0:1].to_broadcast([P, 2 * DM]), ALU.mult).then_inc(raw_high, 1)
                    pool.wait_ge(raw_high, 2 * count + j + 2)
                    last = pool.tensor_tensor(low, raw, f32(high), ALU.subtract)
                last.then_inc(split_done[i], 1)

            def step(p, last=False):
                for c in range(PER_STEP):
                    n = PER_STEP * p + c
                    for i in range(FK0):
                        pool.wait_ge(high_ready, FK0 * n + i + 1)
                        pool.tensor_tensor(hT[c % 2][1][:, i, :], square[:, i, :], f32(hT[c % 2][0][:, i, :]),
                                           ALU.subtract).then_inc(low_ready, 1)
                    if c == 1 and not (isinstance(p, int) and p == 0):
                        pool.wait_ge(down_ready, 2 * PER_STEP * p)
                        split_weights(1, p, 2 * p + 1)
                    if c == CHUNKS + 1 and not last:
                        pool.wait_ge(down_ready, 2 * (PER_STEP * p + CHUNKS))
                        split_weights(0, p + 1, 2 * p + 2)

            split_weights(0, 0, 0)
            split_weights(1, 0, 1)
            step(0)
            with pool.Fori(1, STEPS - 1) as p:
                step(p)
            step(STEPS - 1, True)

        @block.tensor
        def _(pe):
            pe.wait_ge(router_split, 1)
            for t in range(TILES):
                for k in range(DK):
                    last = split_matmul(pe, down_bank[0][:, t * E0:(t + 1) * E0], both(xnT, slice(None), k, slice(t * P, (t + 1) * P)),
                                        both(router, slice(None), k), k == 0, k == DK - 1)
            last.then_inc(logits_ready, 1)

            def up(p, c):
                n = PER_STEP * p + c
                for i in range(FK0):
                    at = 2 * (c % 2) + i
                    if not isinstance(n, int) or n >= 2:
                        pe.wait_ge(square_ready, FK0 * (n - 2) + i + 1)
                    tokens = c % CHUNKS
                    for k in range(DK):
                        last = split_matmul(pe, up_bank[at][:, :], both(fc[c // CHUNKS], slice(None), k, slice(i * P, (i + 1) * P)),
                                            both(xnT, slice(None), k, slice(tokens * SEQ, (tokens + 1) * SEQ)), k == 0, k == DK - 1)
                    last.then_inc(up_ready, 1)

            def down(p, c):
                n = PER_STEP * p + c
                pe.wait_ge(low_ready, FK0 * (n + 1))
                for half in range(2):
                    if not isinstance(n, int) or n >= 2:
                        pe.wait_ge(down_read, 2 * (n - 2) + half + 1)
                    elif n == 0:
                        pe.wait_ge(combine_ready, 1)
                    for t in (2 * half, 2 * half + 1):
                        for i in range(FK0):
                            last = split_matmul(pe, down_bank[2 * (c % 2) + half][:, t % 2 * DM:(t % 2 + 1) * DM],
                                                both(hT[c % 2], slice(None), i, slice(t * P, (t + 1) * P)),
                                                both(proj[c // CHUNKS], slice(None), i), i == 0, i == FK0 - 1)
                    last.then_inc(down_ready, 1)

            def step(p):
                for c in range(PER_STEP):
                    if c % CHUNKS == 0:
                        pe.wait_ge(split_done[c // CHUNKS], p + 1)
                    up(p, c)
                    if c:
                        down(p, c - 1)
                    elif not isinstance(p, int) or p > 0:
                        down(p - 1, PER_STEP - 1)

            step(0)
            with pe.Fori(1, STEPS) as p:
                step(p)
            down(STEPS - 1, PER_STEP - 1)

        @block.scalar
        def _(act):
            act.wait_ge(router_loaded, 16)
            act.copy(router[0][:, :, :], router_raw[:, :, :]).then_inc(router_high, 1)
            act.wait_ge(gap_ready, 1)
            act.activation(gap[:, :], gap[:, :], ACT.Exp).then_inc(exp_ready, 1)

            def chunk(p, c):
                n = PER_STEP * p + c
                for i in range(FK0):
                    act.wait_ge(up_ready, FK0 * n + i + 1)
                    if not isinstance(n, int) or n >= 1:
                        act.wait_ge(square_ready, FK0 * (n - 1) + i + 1)
                    act.activation(relu[:, i, :], up_bank[2 * (c % 2) + i][:, :], ACT.Relu).then_inc(relu_ready, 1)
                for i in range(FK0):
                    act.wait_ge(square_ready, FK0 * n + i + 1)
                    if not isinstance(n, int) or n >= 2:
                        act.wait_ge(down_ready, 2 * (n - 1))
                    act.copy(hT[c % 2][0][:, i, :], square[:, i, :]).then_inc(high_ready, 1)

            def step(p):
                for c in range(PER_STEP):
                    chunk(p, c)

            step(0)
            with act.Fori(1, STEPS) as p:
                step(p)

        @block.vector
        def _(dve):
            count = [0]

            def mine(instruction):
                count[0] += 1
                instruction.then_inc(chain, 1)
                dve.wait_ge(chain, count[0])

            dve.wait_ge(router_high, 1)
            dve.tensor_tensor(router[1][:, :, :], router_raw[:, :, :], f32(router[0][:, :, :]), ALU.subtract).then_inc(router_split, 1)
            dve.wait_ge(logits_ready, 1)
            mine(dve.tensor_copy(logits[:, :, :].rearrange("p t e -> p (t e)"), down_bank[0][:, 0:TILES * E0]))
            for t in range(TILES):
                last = dve.max(top[:, t, :], logits[:, t, :])
            mine(last)
            for t in range(TILES):
                last = dve.max_index(top_at[:, t, :], top[:, t, :], logits[:, t, :])
            mine(last)
            dve.tensor_tensor(gap[:, :], top[:, :, 1], top[:, :, 0], ALU.subtract).then_inc(gap_ready, 1)
            mine(dve.tensor_copy(top_id[:, :, 0:2], top_at[:, :, 0:2]))
            dve.wait_ge(ids_ready, 1)
            ids = expert_id[:, :].rearrange("p (a e) -> p a e", a=1).to_broadcast([P, TILES, E0])
            hits = [hit[:, j, :].rearrange("p (t e) -> p t e", e=E0) for j in range(2)]
            for j in range(2):
                dve.tensor_tensor(hits[j], ids, top_id[:, :, j:j + 1].to_broadcast([P, TILES, E0]), ALU.is_equal)
            dve.wait_ge(exp_ready, 1)
            mine(dve.tensor_scalar(share[:, 1, :], gap[:, :], 1.0, None, ALU.add))
            mine(dve.reciprocal(share[:, 0, :], share[:, 1, :]))
            mine(dve.tensor_tensor(share[:, 1, :], gap[:, :], share[:, 0, :], ALU.mult))
            for j in range(2):
                last = dve.tensor_tensor(hits[j], hits[j], share[:, j, :].rearrange("p (t a) -> p t a", a=1).to_broadcast([P, TILES, E0]), ALU.mult)
            mine(last)
            dve.tensor_tensor(combine[:, :, :], hits[0], hits[1], ALU.add).then_inc(combine_ready, 1)

            def squares(p, c):
                n = PER_STEP * p + c
                for i in range(FK0):
                    dve.wait_ge(relu_ready, FK0 * n + i + 1)
                    if not isinstance(n, int) or n >= 1:
                        dve.wait_ge(low_ready, FK0 * (n - 1) + i + 1)
                    dve.tensor_tensor(square[:, i, :], up_bank[2 * (c % 2) + i][:, :], relu[:, i, :], ALU.mult).then_inc(square_ready, 1)

            def outputs(p, c):
                n = PER_STEP * p + c
                e = 2 * p + c // CHUNKS
                for half in range(2):
                    dve.wait_ge(down_ready, 2 * n + half + 1)
                    for t in (2 * half, 2 * half + 1):
                        tile = c % CHUNKS * BT + t
                        last = dve.scalar_tensor_tensor(x_sb[:, tile, :], down_bank[2 * (c % 2) + half][:, t % 2 * DM:(t % 2 + 1) * DM],
                                                        combine[:, tile, bass.ds(e, 1)], x_sb[:, tile, :], ALU.mult, ALU.add)
                    last.then_inc(down_read, 1)

            def step(p):
                for c in range(PER_STEP):
                    squares(p, c)
                    if c:
                        outputs(p, c - 1)
                    elif not isinstance(p, int) or p > 0:
                        outputs(p - 1, PER_STEP - 1)

            dve.wait_ge(combine_ready, 1)
            step(0)
            with dve.Fori(1, STEPS) as p:
                step(p)
            outputs(STEPS - 1, PER_STEP - 1)

H1, DH1 = 16, 16
HALF = P // DH1
HALVES = 2 * BATCH
PRODUCTS = [(0, 0), (0, 1), (1, 0), (1, 1), (0, 2), (2, 0), (1, 2), (2, 1)]
SCALE1 = 1.0 / float(np.sqrt(np.float32(DH1)))


def project1_phase(nc, xnT, w_qkv, parts_dram, values):
    with ExitStack() as ctx:
        m = Memory(nc, ctx, "p1")
        raw = m.sb("raw", [P, DK, 3 * DM])
        w = m.pair("w", [P, DK, 3 * DM])
        parts = m.sb("parts", [P, 4, 3, SEQ], BF16)
        rest = m.sb("rest", [P, 3, SEQ])
        bank = [m.ps(f"bank{i}") for i in range(6)]
        raw_loaded, w_high, w_split = m.sem("raw_loaded"), m.sem("w_high"), m.sem("w_split")
        proj_ready, first, rest_ready, second, third = (m.sem(n) for n in ("proj_ready", "first", "rest_ready", "second", "third"))
        values_read = m.sem("values_read")
        stored = [m.sem(f"stored{i}") for i in range(4)]
        block = ctx.enter_context(nc.Block())
        PER_BATCH = 6
        QK = [(which, half) for half in range(2) for which in range(2)]

        @block.sync
        def _(sp):
            sp.dma_start(raw[:, :, :], w_qkv.rearrange("(k p) n -> p k n", p=P)).then_inc(raw_loaded, 16)
            for n in range(4 * BATCH):
                b, (which, half) = n // 4, QK[n % 4]
                sp.wait_ge(third, n + 1)
                sp.wait_ge(second, n + 1)
                sp.dma_start(parts_dram[which, :, b, half * P:(half + 1) * P, :].rearrange("s r t -> r s t"),
                             parts[:, n % 4, :, :]).then_inc(stored[n % 4], 16)
            for i in range(4):
                sp.wait_ge(stored[i], 16 * BATCH)

        @block.tensor
        def _(pe):
            pe.wait_ge(w_split, 1)
            for b in range(BATCH):
                for j in range(2):
                    if b:
                        pe.wait_ge(values_read, 2 * b + j - 1)
                    for t in (2 * j, 2 * j + 1):
                        at = b * SEQ + t * P
                        for k in range(DK):
                            last = split_matmul(pe, bank[j][:, t % 2 * DM:(t % 2 + 1) * DM], both(xnT, slice(None), k, slice(at, at + P)),
                                                both(w, slice(None), k, slice(2 * DM, 3 * DM)), k == 0, k == DK - 1)
                    last.then_inc(proj_ready, 1)
                for j, (which, half) in enumerate(QK):
                    if b:
                        pe.wait_ge(rest_ready, 4 * (b - 1) + j + 1)
                    at = which * DM + half * P
                    for k in range(DK):
                        last = split_matmul(pe, bank[2 + j][:, :], both(w, slice(None), k, slice(at, at + P)),
                                            both(xnT, slice(None), k, slice(b * SEQ, (b + 1) * SEQ)), k == 0, k == DK - 1)
                    last.then_inc(proj_ready, 1)

        @block.scalar
        def _(act):
            def second_part(n):
                act.wait_ge(rest_ready, n + 1)
                act.copy(parts[:, n % 4, 1, :], rest[:, n % 3, :]).then_inc(second, 1)

            act.wait_ge(raw_loaded, 16)
            act.copy(w[0][:, :, :], raw[:, :, :]).then_inc(w_high, 1)
            for b in range(BATCH):
                for j in range(2):
                    act.wait_ge(proj_ready, PER_BATCH * b + j + 1)
                    for t in range(2):
                        out = values[:, 2 * b:2 * b + 2, 2 * j + t, :]
                        last = act.copy(out, bank[j][:, t * DM:(t + 1) * DM].rearrange("p (h d) -> p h d", h=2))
                    last.then_inc(values_read, 1)
                for j in range(4):
                    n = 4 * b + j
                    act.wait_ge(proj_ready, PER_BATCH * b + 2 + j + 1)
                    if n >= 4:
                        act.wait_ge(stored[n % 4], 16 * (n // 4))
                    act.copy(parts[:, n % 4, 0, :], bank[2 + j][:, :]).then_inc(first, 1)
                    if n:
                        second_part(n - 1)
            second_part(4 * BATCH - 1)

        @block.vector
        def _(dve):
            dve.wait_ge(w_high, 1)
            dve.tensor_tensor(w[1][:, :, :], raw[:, :, :], f32(w[0][:, :, :]), ALU.subtract).then_inc(w_split, 1)

            def third_part(n):
                dve.wait_ge(second, n + 1)
                dve.tensor_tensor(parts[:, n % 4, 2, :], rest[:, n % 3, :], parts[:, n % 4, 1, :], ALU.subtract).then_inc(third, 1)

            for n in range(4 * BATCH):
                dve.wait_ge(first, n + 1)
                if n >= 3:
                    dve.wait_ge(third, n - 2)
                dve.tensor_tensor(rest[:, n % 3, :], bank[2 + n % 4][:, :], parts[:, n % 4, 0, :], ALU.subtract).then_inc(rest_ready, 1)
                if n:
                    third_part(n - 1)
            third_part(4 * BATCH - 1)


def attention1_phase(nc, x_sb, parts_dram, values, ident, ident_bf, causal_bf, w_out):
    with ExitStack() as ctx:
        m = Memory(nc, ctx, "a1")
        qs = m.sb("qs", [P, 2 * HALF * SEQ], BF16)
        ks = m.sb("ks", [P, 2 * HALF * SEQ], BF16)
        GAP = BT * P + DH1
        placed = tuple(m.sb(n, [P, HALF * GAP], F32R) for n in ("placed_hi", "placed_lo"))
        w_raw = m.sb("w_raw", [P, 2, DM])
        w_pair = m.pair("w", [P, 2, DM])
        probs = [m.sb(f"probs{i}", [P, CAUSAL]) for i in range(4)]
        pT = [m.pair(f"pT{i}", [P, CAUSAL]) for i in range(2)]
        oT = m.pair("oT", [P, SEQ])
        peak = m.sb("peak", [P, 2, BT])
        shift = m.sb("shift", [P, 2, BT])
        total = m.sb("total", [P, 2, BT])
        inverse = m.sb("inverse", [P, 2, BT])
        score_bank = [m.ps(f"score{i}") for i in range(3)]
        turn_bank = [m.ps(f"turn{i}") for i in range(3)]
        out_bank = m.ps("out")
        proj_bank = m.ps("proj")

        w_loaded, w_high, w_split = m.sem("w_loaded"), m.sem("w_high"), m.sem("w_split")
        stacks_loaded, zeroed, values_placed, placed_high = (m.sem(n) for n in ("stacks_loaded", "zeroed", "values_placed", "placed_high"))
        scores_ready, peaks, shift_ready = m.sem("scores_ready"), m.sem("peaks"), m.sem("shift_ready")
        exp_done, inverse_ready, probs_ready = m.sem("exp_done"), m.sem("inverse_ready"), m.sem("probs_ready")
        turn_ready, turn_high, turn_read = m.sem("turn_ready"), m.sem("turn_high"), m.sem("turn_read")
        weighed = m.sem("weighed")
        out_high, out_read = m.sem("out_high"), m.sem("out_read")
        proj_ready, proj_read = m.sem("proj_ready"), m.sem("proj_read")

        SCORE_TILES = [[(0, 0), (2, P)], [(1, 0)], [(3, 0)]]
        STAT = {0: 0, 2: 1, 1: 2, 3: 3}
        STATS_OF_BANK = [(0, 2), (2, 3), (3, 4)]
        TURN_TILES = [[0], [1], [2, 3]]
        STACK_DMAS = 2 * len(PRODUCTS)
        block = ctx.enter_context(nc.Block())

        @block.sync
        def _(sp):
            sp.dma_start(w_raw[:, :, :], w_out.rearrange("(k p) n -> p k n", p=P)).then_inc(w_loaded, 16)

            def load(s):
                for which, stack in enumerate((qs, ks)):
                    for row, product in enumerate(PRODUCTS):
                        src = parts_dram[which, product[which]].rearrange("b (f h d) t -> d (b f) h t", f=2, d=DH1)
                        out = stack[row * DH1:(row + 1) * DH1, bass.ds((s % 2) * (HALF * SEQ), HALF * SEQ)]
                        sp.dma_start(out.rearrange("p (a h t) -> p a h t", a=1, h=HALF), src[:, bass.ds(s, 1), :, :]).then_inc(stacks_loaded, 16)

            load(0)
            sp.wait_ge(stacks_loaded, 16 * STACK_DMAS)
            load(1)
            with sp.Fori(2, HALVES) as s:
                sp.wait_ge(stacks_loaded, 16 * STACK_DMAS * s)
                sp.wait_ge(scores_ready, 3 * HALF * (s - 1))
                load(s)

        @block.gpsimd
        def _(pool):
            for t in placed:
                pool.memset(t[:, :].bitcast(F32), 0.0).then_inc(zeroed, 1)

            def normalize(s, u):
                pool.wait_ge(inverse_ready, HALF * s + u + 1)
                for i in range(BT):
                    rows = probs[u % 4][:, TRI[i]:TRI[i] + (i + 1) * P]
                    by = inverse[:, u % 2, STAT[i]:STAT[i] + 1]
                    if i == 0:
                        last = pool.tensor_tensor(rows, rows, by.to_broadcast([P, P]), ALU.mult)
                    else:
                        last = pool.tensor_scalar(rows, rows, by, 1.0, ALU.mult, ALU.mult)
                last.then_inc(probs_ready, 1)

            with pool.Fori(0, HALVES) as s:
                for u in range(HALF):
                    normalize(s, u)

        @block.tensor
        def _(pe):
            def scores(s, u, bank):
                at = ((s + u // HALF) % 2) * (HALF * SEQ) + u % HALF * SEQ
                for i, col in SCORE_TILES[bank]:
                    out = score_bank[bank][:, col:col + (i + 1) * P]
                    pe.matmul(out, qs[:, bass.ds(at + i * P, P)], ks[:, bass.ds(at, (i + 1) * P)], start=True, stop=False)
                    last = pe.matmul(out[:, i * P:], ident_bf[:, :], causal_bf[:, :], start=False, stop=True)
                last.then_inc(scores_ready, 1)

            def turn(v, group):
                col = 0
                for k in TURN_TILES[group]:
                    for i in range(k, BT):
                        last = pe.transpose(turn_bank[group][:, col:col + P],
                                            probs[v % 4][:, TRI[i] + k * P:TRI[i] + (k + 1) * P], ident[:, :])
                        col += P
                last.then_inc(turn_ready, 1)

            def weigh(w, k):
                at = w * BT * P + k * P
                return split_matmul(pe, out_bank[:, k * P:], both(placed, slice(None), slice(at, at + P)),
                                    both(pT[w % 2], slice(None), slice(KEY_AT[k], KEY_AT[k] + (BT - k) * P)),
                                    w == 0 and k == 0, w == HALF - 1 and k == BT - 1)

            def project(s, j):
                for t in (2 * j, 2 * j + 1):
                    last = split_matmul(pe, proj_bank[:, t % 2 * DM:(t % 2 + 1) * DM], both(oT, slice(None), slice(t * P, (t + 1) * P)),
                                        tuple(x[:, bass.ds(s % 2, 1), :].rearrange("p a d -> p (a d)") for x in w_pair), True, True)
                last.then_inc(proj_ready, 1)

            def slot(s, w, last=False):
                v, u = w + 1, w + 3
                g = HALF * s + w
                turning, scoring = not (last and v >= HALF), not (last and u >= HALF)
                first = isinstance(s, int) and s == 0
                for bank in range(3):
                    if turning:
                        if bank == 0:
                            pe.wait_ge(probs_ready, g + 2)
                        pe.wait_ge(turn_read, 3 * g + bank + 1)
                        turn(v, bank)
                    if scoring:
                        if bank == 0 and u == HALF:
                            pe.wait_ge(stacks_loaded, 16 * STACK_DMAS * (s + 2))
                        pe.wait_ge(exp_done, 3 * g + bank + 7)
                        scores(s, u, bank)
                if w == 0 and not first:
                    pe.wait_ge(out_read, s)
                    project(s - 1, 0)
                if w == 1 and not first:
                    pe.wait_ge(proj_read, 2 * s - 1)
                    project(s - 1, 1)
                pe.wait_ge(turn_read, 3 * g + 3)
                if w % (HALF // 2) == 0:
                    pe.wait_ge(values_placed, 2 * s + 1 + w // (HALF // 2))
                for k in range(BT):
                    done = weigh(w, k)
                done.then_inc(weighed, 1)

            pe.wait_ge(stacks_loaded, 16 * STACK_DMAS)
            for u in range(3):
                for bank in range(3):
                    if u == 2:
                        if bank == 0:
                            pe.wait_ge(probs_ready, 1)
                        turn(0, bank)
                    if u:
                        pe.wait_ge(exp_done, 3 * (u - 1) + bank + 1)
                    scores(0, u, bank)
            pe.wait_ge(zeroed, 2)
            pe.wait_ge(w_split, 1)
            for w in range(HALF):
                slot(0, w)
            with pe.Fori(1, HALVES - 1) as s:
                for w in range(HALF):
                    slot(s, w)
            for w in range(HALF):
                slot(HALVES - 1, w, last=True)
            pe.wait_ge(out_read, HALVES)
            project(HALVES - 1, 0)
            pe.wait_ge(proj_read, 2 * HALVES - 1)
            project(HALVES - 1, 1)

        @block.scalar
        def _(act):
            def exps(s, u, bank):
                act.wait_ge(shift_ready, 3 * (HALF * s + u) + bank + 1)
                for i, col in SCORE_TILES[bank]:
                    c = STAT[i]
                    last = act.activation(probs[u % 4][:, TRI[i]:TRI[i] + (i + 1) * P], score_bank[bank][:, col:col + (i + 1) * P],
                                          ACT.Exp, bias=shift[:, u % 2, c:c + 1], scale=SCALE1, accum_out=total[:, u % 2, c:c + 1])
                last.then_inc(exp_done, 1)

            def turned(s, v, group):
                g = HALF * s + v
                act.wait_ge(turn_ready, 3 * g + group + 1)
                if group == 0 and not (isinstance(g, int) and g < 2):
                    act.wait_ge(weighed, g - 1)
                at = KEY_AT[TURN_TILES[group][0]]
                width = sum((BT - k) * P for k in TURN_TILES[group])
                act.copy(pT[v % 2][0][:, at:at + width], turn_bank[group][:, 0:width]).then_inc(turn_high, 1)

            def slot(s, w, last=False):
                v, u = w + 1, w + 3
                turning, scoring = not (last and v >= HALF), not (last and u >= HALF)
                if turning:
                    turned(s, v, 1)
                    turned(s, v, 2)
                if scoring:
                    exps(s, u, 0)
                    exps(s, u, 1)
                if not (last and v + 1 >= HALF):
                    turned(s, v + 1, 0)
                if scoring:
                    exps(s, u, 2)
                if w == HALF - 1:
                    act.wait_ge(weighed, HALF * (s + 1))
                    act.copy(oT[0][:, :], out_bank[:, :]).then_inc(out_high, 1)

            act.wait_ge(w_loaded, 16)
            act.copy(w_pair[0][:, :, :], w_raw[:, :, :]).then_inc(w_high, 1)
            for u in range(2):
                for bank in range(3):
                    exps(0, u, bank)
            for bank in range(3):
                turned(0, 0, bank)
            exps(0, 2, 0)
            exps(0, 2, 1)
            turned(0, 1, 0)
            exps(0, 2, 2)
            for w in range(HALF):
                slot(0, w)
            with act.Fori(1, HALVES - 1) as s:
                for w in range(HALF):
                    slot(s, w)
            for w in range(HALF):
                slot(HALVES - 1, w, last=True)

        @block.vector
        def _(dve):
            def place(s, half, count):
                heads = slice(half * HALF // 2, (half + 1) * HALF // 2)
                src = values[:, bass.ds(s, 1), :, :].rearrange("p a k (h d) -> p h (a k) d", h=HALF)[:, heads]
                high, low = (t[:, :].rearrange("p (h g) -> p h g", h=HALF)[:, heads, 0:BT * P].rearrange("p h (k c) -> p h k c", k=BT)[:, :, :, 0:DH1] for t in placed)
                dve.tensor_scalar(high, src, 1.0, None, ALU.mult).then_inc(placed_high, 1)
                dve.wait_ge(placed_high, count + 1)
                dve.tensor_tensor(low, src, f32(high), ALU.subtract).then_inc(values_placed, 1)

            def peak_of(s, u, bank):
                g = HALF * s + u
                dve.wait_ge(scores_ready, 3 * g + bank + 1)
                for i, col in SCORE_TILES[bank]:
                    c = STAT[i]
                    last = dve.reduce_max(peak[:, u % 2, c:c + 1], score_bank[bank][:, col:col + (i + 1) * P], AX.X)
                last.then_inc(peaks, 1)
                dve.wait_ge(peaks, 3 * g + bank + 1)
                lo, hi = STATS_OF_BANK[bank]
                dve.tensor_scalar(shift[:, u % 2, lo:hi], peak[:, u % 2, lo:hi], -SCALE1, None, ALU.mult).then_inc(shift_ready, 1)

            def invert(s, u):
                g = HALF * s + u
                dve.wait_ge(exp_done, 3 * g + 3)
                dve.reciprocal(inverse[:, u % 2, :], total[:, u % 2, :]).then_inc(inverse_ready, 1)

            def turned(s, v, group):
                dve.wait_ge(turn_high, 3 * (HALF * s + v) + group + 1)
                at = KEY_AT[TURN_TILES[group][0]]
                width = sum((BT - k) * P for k in TURN_TILES[group])
                dve.tensor_tensor(pT[v % 2][1][:, at:at + width], turn_bank[group][:, 0:width],
                                  f32(pT[v % 2][0][:, at:at + width]), ALU.subtract).then_inc(turn_read, 1)

            def add_projected(s, j):
                dve.wait_ge(proj_ready, 2 * s + j + 1)
                rows = x_sb[:, bass.ds(s // 2 * BT + 2 * j, 2), :].rearrange("p t d -> p (t d)")
                dve.tensor_tensor(rows, proj_bank[:, :], rows, ALU.add).then_inc(proj_read, 1)

            def slot(s, w, last=False):
                v, u = w + 1, w + 3
                turning, scoring = not (last and v >= HALF), not (last and u >= HALF)
                first = isinstance(s, int) and s == 0
                if not (last and u > HALF):
                    invert(s, u - 1)
                if turning:
                    turned(s, v, 1)
                if scoring:
                    peak_of(s, u, 0)
                if turning:
                    turned(s, v, 2)
                if scoring:
                    peak_of(s, u, 1)
                    peak_of(s, u, 2)
                if not (last and v + 1 >= HALF):
                    turned(s, v + 1, 0)
                if w in (0, 1) and not first:
                    add_projected(s - 1, w)
                if w == 2 and not first:
                    dve.wait_ge(weighed, HALF * s)
                    place(s, 1, 2 * s + 1)
                if w == HALF // 2 + 1 and not last:
                    dve.wait_ge(weighed, HALF * s + HALF // 2)
                    place(s + 1, 0, 2 * s + 2)
                if w == HALF - 1:
                    dve.wait_ge(out_high, s + 1)
                    dve.tensor_tensor(oT[1][:, :], out_bank[:, :], f32(oT[0][:, :]), ALU.subtract).then_inc(out_read, 1)

            dve.wait_ge(w_high, 1)
            dve.tensor_tensor(w_pair[1][:, :, :], w_raw[:, :, :], f32(w_pair[0][:, :, :]), ALU.subtract).then_inc(w_split, 1)
            dve.wait_ge(zeroed, 2)
            place(0, 0, 0)
            place(0, 1, 1)
            for u in range(2):
                for bank in range(3):
                    peak_of(0, u, bank)
                if u == 0:
                    invert(0, 0)
            invert(0, 1)
            for bank in range(3):
                turned(0, 0, bank)
                peak_of(0, 2, bank)
            turned(0, 1, 0)
            for w in range(HALF):
                slot(0, w)
            with dve.Fori(1, HALVES - 1) as s:
                for w in range(HALF):
                    slot(s, w)
            for w in range(HALF):
                slot(HALVES - 1, w, last=True)
            for j in range(2):
                add_projected(HALVES - 1, j)

E1, DF1 = 16, 176
REST1 = DF1 - P
SLOT_TILES = 2 * TILES + E1
RING1 = 4


def past(s, n):
    return not isinstance(s, int) or s >= n


def begin_zero_rows(nc, zero_row, rows_dram, rows_zeroed):
    with ExitStack() as ctx:
        m = Memory(nc, ctx, "zr")
        zero_ready = m.sem("zero_ready")
        block = ctx.enter_context(nc.Block())

        @block.gpsimd
        def _(pool):
            pool.memset(zero_row[:, :, :], 0.0).then_inc(zero_ready, 1)

        @block.sync
        def _(sp):
            sp.wait_ge(zero_ready, 1)
            sp.dma_start(rows_dram.rearrange("(s p) d -> p s d", p=P),
                         zero_row[:, :, :].to_broadcast([P, SLOT_TILES, DM])).then_inc(rows_zeroed, 16)


def begin_expert_loads(nc, w13, w2, w1_dram, w3_dram, w2_dram, w13_loaded, w2_loaded):
    with ExitStack() as ctx:
        block = ctx.enter_context(nc.Block())

        @block.sync
        def _(sp):
            for i, w in enumerate((w1_dram, w3_dram)):
                for k in range(DK):
                    sp.dma_start(f32(w13[:, :, k, i * DF1:(i + 1) * DF1]), w[:, k * P:(k + 1) * P, :].rearrange("e p n -> p e n")).then_inc(w13_loaded, 16)
            sp.dma_start(f32(w2[:, :, 0, :]), w2_dram[:, 0:P, :].rearrange("e p n -> p e n")).then_inc(w2_loaded, 16)
            sp.dma_start(f32(w2[0:REST1, :, 1, :]), w2_dram[:, P:DF1, :].rearrange("e p n -> p e n")).then_inc(w2_loaded, 16)


def route1_phase(nc, xnT, gate_w, slot_of, share, expert_of):
    with ExitStack() as ctx:
        m = Memory(nc, ctx, "r1")
        raw = m.sb("raw", [P, DK, E1])
        router = m.pair("router", [P, DK, E1])
        before = m.sb("before", [P, P], BF16)
        ones = m.sb("ones", [P, P], BF16)
        ids = m.sb("ids", [P, E1])
        full = m.sb("full", [P, TILES])
        tile_ids = m.sb("tile_ids", [P, SLOT_TILES])
        probs = m.sb("probs", [P, TILES, E1])
        stat = m.sb("stat", [P, 2, TILES])
        top = m.sb("top", [P, TILES, 8])
        top_at = m.sb("top_at", [P, TILES, 8], mybir.dt.uint32)
        top_id = m.sb("top_id", [P, TILES, 2])
        hit = m.sb("hit", [P, 2, TILES * E1])
        hits_bf = m.sb("hits_bf", [P, TILES * E1], BF16)
        square = m.sb("square", [P, E1, E1])
        order = m.sb("order", [P, E1, E1])
        tiles_of = m.sb("tiles_of", [P, E1])
        tiles_to = m.sb("tiles_to", [P, E1])
        base = m.sb("base", [P, E1])
        slots = m.sb("slots", [P, TILES, E1])
        picked = m.sb("picked", [P, 2, TILES * E1])
        slot_f = m.sb("slot_f", [P, 2, TILES])
        ended = m.sb("ended", [P, SLOT_TILES, E1])
        expert_f = m.sb("expert_f", [P, SLOT_TILES])
        logit_bank, rank_bank, count_bank = m.ps("logit"), m.ps("rank"), m.ps("count")
        raw_loaded, router_high, router_split = m.sem("raw_loaded"), m.sem("router_high"), m.sem("router_split")
        logits_ready, shifted, exp_ready, hits_ready, counted = (m.sem(n) for n in ("logits_ready", "shifted", "exp_ready", "hits_ready", "counted"))
        filled, tables_ready, chain = m.sem("filled"), m.sem("tables_ready"), m.sem("chain")
        block = ctx.enter_context(nc.Block())

        @block.sync
        def _(sp):
            sp.dma_start(raw[:, :, :], gate_w.rearrange("(k p) e -> p k e", p=P)).then_inc(raw_loaded, 16)

        @block.gpsimd
        def _(pool):
            pool.memset(ones[:, :], 1.0).then_inc(tables_ready, 1)
            pool.memset(before[:, :], 1.0).then_inc(filled, 1)
            for t, step, n in ((ids, 1, E1), (full, P, TILES), (tile_ids, 1, SLOT_TILES)):
                pool.iota(t[:, :], pattern=[[step, n]], base=0, channel_multiplier=0,
                          allow_small_or_imprecise_dtypes=True).then_inc(tables_ready, 1)
            pool.wait_ge(filled, 1)
            pool.affine_select(out=before[:, :], in_=before[:, :], compare_op=ALU.is_gt, fill=0.0, base=0,
                               pattern=[[1, P]], channel_multiplier=-1).then_inc(tables_ready, 1)

        @block.tensor
        def _(pe):
            pe.wait_ge(router_split, 1)
            for t in range(TILES):
                for k in range(DK):
                    last = split_matmul(pe, logit_bank[:, t * E1:(t + 1) * E1], both(xnT, slice(None), k, slice(t * P, (t + 1) * P)),
                                        both(router, slice(None), k), k == 0, k == DK - 1)
            last.then_inc(logits_ready, 1)
            pe.wait_ge(tables_ready, 5)
            pe.wait_ge(hits_ready, 1)
            every = TILES * E1
            pe.matmul(rank_bank[:, 0:every], before[:, :], hits_bf[:, :], start=True, stop=False)
            for s in range(1, TILES):
                pe.matmul(rank_bank[:, s * E1:every], ones[:, :], hits_bf[:, 0:every - s * E1], start=False, stop=s == TILES - 1)
            for t in range(TILES):
                last = pe.matmul(count_bank[:, 0:E1], ones[:, :], hits_bf[:, t * E1:(t + 1) * E1], start=t == 0, stop=t == TILES - 1)
            last.then_inc(counted, 1)

        @block.scalar
        def _(act):
            act.wait_ge(raw_loaded, 16)
            act.copy(router[0][:, :, :], raw[:, :, :]).then_inc(router_high, 1)
            act.wait_ge(shifted, 1)
            act.activation(probs[:, :, :], probs[:, :, :], ACT.Exp).then_inc(exp_ready, 1)

        @block.vector
        def _(dve):
            count = [0]

            def mine(instruction):
                count[0] += 1
                instruction.then_inc(chain, 1)
                dve.wait_ge(chain, count[0])

            def down(ap, n, inner):
                return ap.rearrange("p (n a) -> p n a", a=1).to_broadcast([P, n, inner])

            def across(ap, outer, n):
                return ap.rearrange("p (a n) -> p a n", a=1).to_broadcast([P, outer, n])

            dve.wait_ge(router_high, 1)
            dve.tensor_tensor(router[1][:, :, :], raw[:, :, :], f32(router[0][:, :, :]), ALU.subtract).then_inc(router_split, 1)
            dve.wait_ge(tables_ready, 5)
            mine(dve.tensor_tensor(order[:, :, :], down(ids[:, :], E1, E1), across(ids[:, :], E1, E1), ALU.is_ge))
            logits = logit_bank[:, 0:TILES * E1].rearrange("p (t e) -> p t e", e=E1)
            dve.wait_ge(logits_ready, 1)
            mine(dve.reduce_max(stat[:, 0, :], logits, AX.X))
            dve.tensor_tensor(probs[:, :, :], logits, down(stat[:, 0, :], TILES, E1), ALU.subtract).then_inc(shifted, 1)
            dve.wait_ge(exp_ready, 1)
            mine(dve.reduce_sum(stat[:, 1, :], probs[:, :, :], AX.X))
            mine(dve.reciprocal(stat[:, 0, :], stat[:, 1, :]))
            mine(dve.tensor_tensor(probs[:, :, :], probs[:, :, :], down(stat[:, 0, :], TILES, E1), ALU.mult))
            for t in range(TILES):
                last = dve.max(top[:, t, :], probs[:, t, :])
            mine(last)
            for t in range(TILES):
                last = dve.max_index(top_at[:, t, :], top[:, t, :], probs[:, t, :])
            mine(last)
            dve.tensor_copy(top_id[:, :, :], top_at[:, :, 0:2])
            mine(dve.tensor_tensor(stat[:, 0, :], top[:, :, 0], top[:, :, 1], ALU.add))
            mine(dve.reciprocal(stat[:, 1, :], stat[:, 0, :]))
            for j in range(2):
                dve.tensor_tensor(share[:, j, :], top[:, :, j], stat[:, 1, :], ALU.mult)
            hits = [hit[:, j, :].rearrange("p (t e) -> p t e", e=E1) for j in range(2)]
            for j in range(2):
                last = dve.tensor_tensor(hits[j], across(ids[:, :], TILES, E1), top_id[:, :, j:j + 1].to_broadcast([P, TILES, E1]), ALU.is_equal)
            mine(last)
            dve.tensor_tensor(hits_bf[:, :], hit[:, 0, :], hit[:, 1, :], ALU.add).then_inc(hits_ready, 1)
            dve.wait_ge(counted, 1)
            mine(dve.tensor_tensor(square[:, :, :], down(count_bank[:, 0:E1], E1, TILES), across(full[:, :], E1, TILES), ALU.is_gt))
            mine(dve.reduce_sum(tiles_of[:, :], square[:, :, :], AX.X))
            mine(dve.tensor_tensor(square[:, :, :], order[:, :, :], across(tiles_of[:, :], E1, E1), ALU.mult))
            mine(dve.reduce_sum(tiles_to[:, :], square[:, :, :], AX.X))
            mine(dve.tensor_tensor(base[:, :], tiles_to[:, :], tiles_of[:, :], ALU.subtract))
            mine(dve.tensor_scalar(base[:, :], base[:, :], float(P), None, ALU.mult))
            ranks = rank_bank[:, 0:TILES * E1].rearrange("p (t e) -> p t e", e=E1)
            mine(dve.tensor_tensor(slots[:, :, :], ranks, across(base[:, :], TILES, E1), ALU.add))
            for j in range(2):
                last = dve.tensor_tensor(picked[:, j, :], hit[:, j, :], slots[:, :, :].rearrange("p t e -> p (t e)"), ALU.mult)
            mine(last)
            mine(dve.reduce_sum(slot_f[:, :, :], picked[:, :, :].rearrange("p j (t e) -> p j t e", e=E1), AX.X))
            dve.tensor_copy(slot_of[:, :, :], slot_f[:, :, :])
            mine(dve.tensor_tensor(ended[:, :, :], down(tile_ids[:, :], SLOT_TILES, E1), across(tiles_to[:, :], SLOT_TILES, E1), ALU.is_ge))
            mine(dve.reduce_sum(expert_f[:, :], ended[:, :, :], AX.X))
            mine(dve.tensor_scalar(expert_f[:, :], expert_f[:, :], float(E1 - 1), None, ALU.min))
            dve.tensor_copy(expert_of[:, :], expert_f[:, :])


def experts1_phase(nc, xn, slot_of, expert_of, rows_dram, outs_dram, rows_zeroed, w13, w2, w13_loaded, w2_loaded, ident):
    with ExitStack() as ctx:
        m = Memory(nc, ctx, "e1")
        rows = m.sb("rows", [P, RING1, DM])
        xT = [m.pair(f"xT{i}", [P, DK * P]) for i in range(2)]
        gate = m.sb("gate", [P, 2, DF1])
        h = m.sb("h", [P, 2, 2 * P])
        hT = [m.pair(f"hT{i}", [P, 2 * P]) for i in range(2)]
        outs = m.sb("outs", [P, RING1, DM])
        x_bank, up_bank, h_bank, down_bank = ([m.ps(f"{n}{i}") for i in range(2)] for n in ("x", "up", "h", "down"))
        scattered = m.sem("scattered")
        w_high, w_split, padded = m.sem("w_high"), m.sem("w_split"), m.sem("padded")
        loaded = [m.sem(f"loaded{i}") for i in range(RING1)]
        stored = [m.sem(f"stored{i}") for i in range(RING1)]
        x_turned, x_high, x_low = m.sem("x_turned"), m.sem("x_high"), m.sem("x_low")
        up_ready, gate_ready, h_ready = m.sem("up_ready"), m.sem("gate_ready"), m.sem("h_ready")
        h_turned, h_high, h_low = m.sem("h_turned"), m.sem("h_high"), m.sem("h_low")
        down_ready, out_ready = m.sem("down_ready"), m.sem("out_ready")
        block = ctx.enter_context(nc.Block())
        STEPS = SLOT_TILES // RING1
        CUT = 4

        def pieces():
            for e in range(0, E1, CUT):
                yield both(w13, slice(None), slice(e, e + CUT)), w13_loaded, 16 * 2 * DK
            for e in range(0, E1, CUT):
                yield both(w2, slice(None), slice(e, e + CUT), 0), w2_loaded, 16 * 2
                yield both(w2, slice(0, REST1), slice(e, e + CUT), 1), w2_loaded, 16 * 2

        def run(eng, tile_step):
            tile_step(0, -1)
            for q in range(2):
                for r in range(RING1):
                    tile_step(q, r)
            with eng.Fori(2, STEPS - 1) as q:
                for r in range(RING1):
                    tile_step(q, r)
            for r in range(RING1 + 2):
                tile_step(STEPS - 1, r)

        def exists(s):
            return not isinstance(s, int) or 0 <= s < SLOT_TILES

        @block.gpsimd
        def _(pool):
            for i in range(2):
                pool.memset(h[:, i, :], 0.0).then_inc(padded, 1)
            pool.wait_ge(rows_zeroed, 16)
            for t in range(TILES):
                for j in range(2):
                    pool.indirect_dma_start(rows_dram[:, :], bass.IndirectOffsetOnAxis(ap=slot_of[:, j, t:t + 1], axis=0),
                                            xn[:, t, :], None).then_inc(scattered, 16)
            pool.wait_ge(scattered, 16 * 2 * TILES)

        @block.sync
        def _(sp):
            def load(q, r):
                s = RING1 * q + r
                if past(s, RING1):
                    sp.wait_ge(x_turned, s - RING1 + 1)
                sp.dma_start(rows[:, r % RING1, :], rows_dram[bass.ds(s * P, P), :]).then_inc(loaded[r % RING1], 16)

            def tile_step(q, r):
                s = RING1 * q + r
                if exists(s + RING1) and not (isinstance(s, int) and s < 0):
                    load(q, r + RING1)
                if exists(s - 2):
                    sp.wait_ge(out_ready, s - 1)
                    sp.dma_start(outs_dram[bass.ds((s - 2) * P, P), :], outs[:, (r - 2) % RING1, :]).then_inc(stored[(r - 2) % RING1], 16)

            sp.wait_ge(scattered, 16 * 2 * TILES)
            for r in range(RING1):
                load(0, r)
            run(sp, tile_step)
            for i in range(RING1):
                sp.wait_ge(stored[i], 16 * STEPS)

        @block.tensor
        def _(pe):
            def expert_at(s):
                return pe.value_load(expert_of[0:1, bass.ds(s, 1)], min_val=0, max_val=E1 - 1)

            def of_expert(pair, rows_, e, k):
                return tuple(t[rows_, bass.ds(e, 1), k, :].rearrange("p a n -> p (a n)") for t in pair)

            def tile_step(q, r):
                s = RING1 * q + r
                if exists(s + 1):
                    pe.wait_ge(loaded[(r + 1) % RING1], 16 * (q + (r + 1) // RING1 + 1))
                    if past(s + 1, 2):
                        pe.wait_ge(x_low, s)
                    for k in range(DK):
                        last = pe.transpose(x_bank[(r + 1) % 2][:, k * P:(k + 1) * P], rows[:, (r + 1) % RING1, k * P:(k + 1) * P], ident[:, :])
                    last.then_inc(x_turned, 1)
                if exists(s):
                    e = expert_at(s)
                    pe.wait_ge(x_low, s + 1)
                    if past(s, 2):
                        pe.wait_ge(h_ready, s - 1)
                    for k in range(DK):
                        last = split_matmul(pe, up_bank[r % 2][:, 0:2 * DF1], both(xT[r % 2], slice(None), slice(k * P, (k + 1) * P)),
                                            of_expert(w13, slice(None), e, k), k == 0, k == DK - 1)
                    last.then_inc(up_ready, 1)
                if exists(s - 1):
                    pe.wait_ge(h_ready, s)
                    if past(s - 1, 2):
                        pe.wait_ge(h_low, s - 2)
                    for k in range(2):
                        last = pe.transpose(h_bank[(r - 1) % 2][:, k * P:(k + 1) * P], h[:, (r - 1) % 2, k * P:(k + 1) * P], ident[:, :])
                    last.then_inc(h_turned, 1)
                if exists(s - 2):
                    e = expert_at(s - 2)
                    pe.wait_ge(h_low, s - 1)
                    if past(s - 2, 2):
                        pe.wait_ge(out_ready, s - 3)
                    for k, rows_ in enumerate((slice(0, P), slice(0, REST1))):
                        last = split_matmul(pe, down_bank[r % 2][:, 0:DM], both(hT[r % 2], rows_, slice(k * P, (k + 1) * P)),
                                            of_expert(w2, rows_, e, k), k == 0, k == 1)
                    last.then_inc(down_ready, 1)

            pe.wait_ge(w_split, len(list(pieces())))
            pe.wait_ge(padded, 2)
            run(pe, tile_step)

        @block.scalar
        def _(act):
            for (high, low), load, count in pieces():
                act.wait_ge(load, count)
                act.copy(high, f32(low)).then_inc(w_high, 1)

            def tile_step(q, r):
                s = RING1 * q + r
                if exists(s + 1):
                    act.wait_ge(x_turned, s + 2)
                    if past(s + 1, 2):
                        act.wait_ge(up_ready, s)
                    act.copy(xT[(r + 1) % 2][0][:, :], x_bank[(r + 1) % 2][:, 0:DK * P]).then_inc(x_high, 1)
                if exists(s):
                    act.wait_ge(up_ready, s + 1)
                    if past(s, 2):
                        act.wait_ge(h_ready, s - 1)
                    act.activation(gate[:, r % 2, :], up_bank[r % 2][:, 0:DF1], ACT.Silu).then_inc(gate_ready, 1)
                if exists(s - 1):
                    act.wait_ge(h_turned, s)
                    if past(s - 1, 2):
                        act.wait_ge(down_ready, s - 2)
                    act.copy(hT[(r - 1) % 2][0][:, :], h_bank[(r - 1) % 2][:, 0:2 * P]).then_inc(h_high, 1)
                if exists(s - 2):
                    act.wait_ge(down_ready, s - 1)
                    if past(s - 2, RING1):
                        act.wait_ge(stored[(r - 2) % RING1], 16 * (q + (r - 2) // RING1))
                    act.copy(outs[:, (r - 2) % RING1, :], down_bank[r % 2][:, 0:DM]).then_inc(out_ready, 1)

            run(act, tile_step)

        @block.vector
        def _(dve):
            for n, ((high, low), _, _) in enumerate(pieces()):
                dve.wait_ge(w_high, n + 1)
                dve.tensor_tensor(low, f32(low), f32(high), ALU.subtract).then_inc(w_split, 1)
            dve.wait_ge(padded, 2)

            def tile_step(q, r):
                s = RING1 * q + r
                if exists(s + 1):
                    dve.wait_ge(x_high, s + 2)
                    dve.tensor_tensor(xT[(r + 1) % 2][1][:, :], x_bank[(r + 1) % 2][:, 0:DK * P], f32(xT[(r + 1) % 2][0][:, :]),
                                      ALU.subtract).then_inc(x_low, 1)
                if exists(s):
                    dve.wait_ge(gate_ready, s + 1)
                    if past(s, 2):
                        dve.wait_ge(h_turned, s - 1)
                    dve.tensor_tensor(h[:, r % 2, 0:DF1], up_bank[r % 2][:, DF1:2 * DF1], gate[:, r % 2, :], ALU.mult).then_inc(h_ready, 1)
                if exists(s - 1):
                    dve.wait_ge(h_high, s)
                    dve.tensor_tensor(hT[(r - 1) % 2][1][:, :], h_bank[(r - 1) % 2][:, 0:2 * P], f32(hT[(r - 1) % 2][0][:, :]),
                                      ALU.subtract).then_inc(h_low, 1)

            run(dve, tile_step)


def combine1_phase(nc, x_sb, slot_of, share, outs_dram, out_dram):
    with ExitStack() as ctx:
        m = Memory(nc, ctx, "c1")
        picked = m.sb("picked", [P, 2, TILES, DM])
        gathered = [m.sem(f"gathered{b}") for b in range(BATCH)]
        first_added, added, stored = m.sem("first_added"), m.sem("added"), m.sem("stored")
        block = ctx.enter_context(nc.Block())

        @block.gpsimd
        def _(pool):
            for t in range(TILES):
                for j in range(2):
                    pool.indirect_dma_start(picked[:, j, t, :], None, outs_dram[:, :],
                                            bass.IndirectOffsetOnAxis(ap=slot_of[:, j, t:t + 1], axis=0)).then_inc(gathered[t // BT], 16)

        @block.vector
        def _(dve):
            for b in range(BATCH):
                dve.wait_ge(gathered[b], 16 * 2 * BT)
                for j in range(2):
                    if j:
                        dve.wait_ge(first_added, BT * (b + 1))
                    for t in range(b * BT, (b + 1) * BT):
                        dve.scalar_tensor_tensor(x_sb[:, t, :], picked[:, j, t, :], share[:, j, t:t + 1], x_sb[:, t, :],
                                                 ALU.mult, ALU.add).then_inc(added if j else first_added, 1)

        @block.sync
        def _(sp):
            for b in range(BATCH):
                sp.wait_ge(added, BT * (b + 1))
                sp.dma_start(out_dram[b].rearrange("(t p) d -> p t d", p=P), x_sb[:, b * BT:(b + 1) * BT, :]).then_inc(stored, 16)
            sp.wait_ge(stored, 16 * BATCH)


def two_layers(nc, x, Wq, bq, Wk, bk, Wv, bv, Wo, bo, w_router, w_fc, w_proj, w_qkv, w_out, gate_w, w1, w3, w2, out):
    with ExitStack() as ctx:
        m = Memory(nc, ctx, "all")
        x_sb = m.sb("x", [P, TILES, DM])
        ident = m.sb("ident", [P, P])
        ident_bf = m.sb("ident_bf", [P, P], BF16)
        causal_bf = m.sb("causal_bf", [P, P], BF16)
        zero_row = m.sb("zero_row", [P, 1, DM])
        slot_of = m.sb("slot_of", [P, 2, TILES], mybir.dt.uint32)
        share = m.sb("share", [P, 2, TILES])
        expert_of = m.sb("expert_of", [P, SLOT_TILES], I32)
        parts_dram = nc.dram_tensor("qk_parts", [2, 3, BATCH, DM, SEQ], BF16, kind="Internal").ap()
        rows_dram = nc.dram_tensor("slot_rows", [SLOT_TILES * P, DM], F32, kind="Internal").ap()
        outs_dram = nc.dram_tensor("slot_outs", [SLOT_TILES * P, DM], F32, kind="Internal").ap()
        rows_zeroed, w13_loaded, w2_loaded = m.sem("rows_zeroed"), m.sem("w13_loaded"), m.sem("w2_loaded")
        ln_signals = [m.sem("ln_" + name) for name in LN_SIGNALS]

        constants_phase(nc, x, x_sb, ident, ident_bf, causal_bf)
        with ExitStack() as layer:
            xnT = Memory(nc, layer, "l0").pair("xnT", [P, DK, TOKENS])
            layernorm_phase(nc, "ln0", ln_signals, 0, x_sb, ident, xnT)
            attention0_phase(nc, x_sb, xnT, ident, ident_bf, causal_bf, Wq, bq, Wk, bk, Wv, bv, Wo, bo)
            begin_zero_rows(nc, zero_row, rows_dram, rows_zeroed)
            layernorm_phase(nc, "ln1", ln_signals, 1, x_sb, ident, xnT)
            moe0_phase(nc, x_sb, xnT, w_router, w_fc, w_proj)
        with ExitStack() as layer:
            values = Memory(nc, layer, "l1").sb("values", [P, HALVES, BT, P])
            with ExitStack() as part:
                xnT = Memory(nc, part, "l1").pair("xnT", [P, DK, TOKENS])
                layernorm_phase(nc, "ln2", ln_signals, 2, x_sb, ident, xnT)
                project1_phase(nc, xnT, w_qkv, parts_dram, values)
            attention1_phase(nc, x_sb, parts_dram, values, ident, ident_bf, causal_bf, w_out)
        with ExitStack() as layer:
            l1 = Memory(nc, layer, "l1f")
            xn = l1.sb("xn", [P, TILES, DM])
            w13_low, w2_low = l1.sb("w13_lo", [P, E1, DK, 2 * DF1], F32R), l1.sb("w2_lo", [P, E1, 2, DM], F32R)
            begin_expert_loads(nc, w13_low, w2_low, w1, w3, w2, w13_loaded, w2_loaded)
            with ExitStack() as part:
                xnT = Memory(nc, part, "l1f").pair("xnT", [P, DK, TOKENS])
                layernorm_phase(nc, "ln3", ln_signals, 3, x_sb, ident, xnT, xn)
                route1_phase(nc, xnT, gate_w, slot_of, share, expert_of)
            w13 = (l1.sb("w13_hi", [P, E1, DK, 2 * DF1], F32R), w13_low)
            w2_pair = (l1.sb("w2_hi", [P, E1, 2, DM], F32R), w2_low)
            experts1_phase(nc, xn, slot_of, expert_of, rows_dram, outs_dram, rows_zeroed, w13, w2_pair,
                           w13_loaded, w2_loaded, ident)
        combine1_phase(nc, x_sb, slot_of, share, outs_dram, out)


_INS = ["L0_attn_x", "L0_attn_Wq", "L0_attn_bq", "L0_attn_Wk", "L0_attn_bk", "L0_attn_Wv", "L0_attn_bv", "L0_attn_Wo",
        "L0_attn_bo", "L0_ffn_w_router", "L0_ffn_w_fc", "L0_ffn_w_proj", "L1_attn_w_qkv", "L1_attn_w_out",
        "L1_ffn_gate_w", "L1_ffn_w1", "L1_ffn_w3", "L1_ffn_w2"]
_OUTS = [((4, 512, 256), "float32")]


def kernel(**inputs):
    import numpy as _np
    import concourse.bacc as _bacc
    from concourse import mybir as _mybir
    from concourse.bass_utils import run_bass_kernel_spmd as _run

    nc = _bacc.Bacc("TRN2", target_bir_lowering=False, num_devices=1)
    arrays, args = {}, []
    for name in _INS:
        a = _np.ascontiguousarray(inputs[name])
        arrays[f"in_{name}_dram"] = a
        args.append(nc.dram_tensor(f"in_{name}_dram", a.shape, _mybir.dt.from_np(a.dtype), kind="ExternalInput").ap())
    for i, (shape, dtype) in enumerate(_OUTS):
        dt = _mybir.dt.from_np(_np.dtype(dtype))
        args.append(nc.dram_tensor(f"out_{i}_dram", shape, dt, kind="ExternalOutput").ap())
    two_layers(nc, *args)
    r = _run(nc, [arrays], core_ids=[0])
    got = tuple(r.results[0][f"out_{i}_dram"] for i in range(len(_OUTS)))
    return got[0]
```

```python
from contextlib import ExitStack

import numpy as np
import concourse.bass as bass
from concourse import mybir

F32 = mybir.dt.float32
F32R = mybir.dt.float32r
BF16 = mybir.dt.bfloat16
I32 = mybir.dt.int32
ALU = mybir.AluOpType
ACT = mybir.ActivationFunctionType
AX = mybir.AxisListType

P = 128
BATCH, SEQ, DM = 4, 512, 256
TOKENS = BATCH * SEQ
TILES = TOKENS // P
BT = SEQ // P
DK = DM // P
LN_EPS = 1e-5
MASKED = -1e30

TRI = [P * i * (i + 1) // 2 for i in range(BT)]
CAUSAL = P * BT * (BT + 1) // 2
KEY_AT = [sum((BT - j) * P for j in range(k)) for k in range(BT)]


def f32(ap):
    return ap.bitcast(F32)


def split_matmul(pe, out, stationary, moving, start, stop):
    (sh, sl), (mh, ml) = stationary, moving
    pe.matmul(out, sh, mh, start=start, stop=False)
    pe.matmul(out, sh, ml, start=False, stop=False)
    return pe.matmul(out, sl, mh, start=False, stop=stop)


class Memory:

    def __init__(self, nc, ctx, tag):
        self.nc, self.ctx, self.tag = nc, ctx, tag

    def sb(self, name, shape, dt=F32):
        return self.ctx.enter_context(self.nc.sbuf_tensor(f"{self.tag}_{name}", shape, dt))

    def pair(self, name, shape):
        return self.sb(name + "_hi", shape, F32R), self.sb(name + "_lo", shape, F32R)

    def ps(self, name, dt=F32, cols=512):
        return self.ctx.enter_context(self.nc.psum_tensor(f"{self.tag}_{name}", [P, cols], dt))

    def sem(self, name):
        return self.ctx.enter_context(self.nc.semaphore(f"{self.tag}_{name}"))


def both(pair, *index):
    return tuple(t[index] for t in pair)


def constants_phase(nc, x_dram, x_loaded, x_sb, ident, ident_bf, causal_bf):
    with ExitStack() as ctx:
        m = Memory(nc, ctx, "cst")
        zeroed, shaped = m.sem("zeroed"), m.sem("shaped")
        block = ctx.enter_context(nc.Block())

        @block.sync
        def _(sp):
            for b in range(BATCH):
                sp.dma_start(x_sb[:, b * BT:(b + 1) * BT, :],
                             x_dram[b].rearrange("(t p) d -> p t d", p=P)).then_inc(x_loaded[b], 16)

        @block.gpsimd
        def _(pool):
            pool.memset(ident[:, :], 0.0).then_inc(zeroed, 1)
            pool.memset(ident_bf[:, :], 0.0).then_inc(zeroed, 1)
            pool.memset(causal_bf[:, :], 0.0).then_inc(zeroed, 1)
            pool.wait_ge(zeroed, 3)
            for t in (ident, ident_bf):
                pool.affine_select(out=t[:, :], in_=t[:, :], compare_op=ALU.not_equal, fill=1.0,
                                   base=0, pattern=[[-1, P]], channel_multiplier=1).then_inc(shaped, 1)
            pool.affine_select(out=causal_bf[:, :], in_=causal_bf[:, :], compare_op=ALU.is_ge,
                               fill=MASKED, base=0, pattern=[[-1, P]],
                               channel_multiplier=1).then_inc(shaped, 1)
            pool.wait_ge(shaped, 3)


LN_SIGNALS = ("chain", "var_ready", "std_ready", "scale_ready", "xn_ready", "turned_ready", "high_ready", "low_ready")
LN_CHAIN = 2 * TILES + BATCH


def layernorm_phase(nc, tag, signals, call, x_sb, ident, xnT, xn_all=None, loads=None, x_loaded=None):
    with ExitStack() as ctx:
        m = Memory(nc, ctx, tag)
        stats = m.sb("stats", [P, TILES, 6])
        moments = m.sb("moments", [P, TILES, 2])
        std = m.sb("std", [P, TILES])
        rstd = m.sb("rstd", [P, TILES])
        offset = m.sb("offset", [P, TILES])
        if xn_all is None:
            places = 2
            xn = m.sb("xn", [P, places, BT, DM])
        else:
            places = BATCH
            xn = xn_all[:, :, :].rearrange("p (b t) d -> p b t d", b=BATCH)
        turned = [m.ps(f"turned{i}") for i in range(4)]
        chain, var_ready, std_ready, scale_ready, xn_ready, turned_ready, high_ready, low_ready = signals
        chained, batches, turns = call * LN_CHAIN, call * BATCH, call * DK * BATCH
        block = ctx.enter_context(nc.Block())

        @block.sync
        def _(sp):
            if loads:
                loads(sp)

        @block.vector
        def _(dve):
            count = [chained]

            def statistics(b):
                tiles = range(b * BT, (b + 1) * BT)
                if x_loaded:
                    dve.wait_ge(x_loaded[b], 16)
                for t in tiles:
                    dve.bn_stats(stats[:, t, :], x_sb[:, t, :]).then_inc(chain, 1)
                for t in tiles:
                    count[0] += 1
                    dve.wait_ge(chain, count[0])
                    dve.bn_aggr(moments[:, t, :], stats[:, t, :]).then_inc(chain, 1)
                count[0] += BT
                dve.wait_ge(chain, count[0])
                cols = slice(b * BT, (b + 1) * BT)
                dve.tensor_scalar(std[:, cols], moments[:, cols, 1], LN_EPS, None, ALU.add).then_inc(var_ready, 1)

            def scales(b):
                cols = slice(b * BT, (b + 1) * BT)
                dve.wait_ge(std_ready, batches + b + 1)
                dve.reciprocal(rstd[:, cols], std[:, cols]).then_inc(chain, 1)
                count[0] += 1
                dve.wait_ge(chain, count[0])
                dve.scalar_tensor_tensor(offset[:, cols], moments[:, cols, 0], -1.0, rstd[:, cols], ALU.mult,
                                         ALU.mult).then_inc(scale_ready, 1)

            def low_parts(b):
                for k in range(DK):
                    dve.wait_ge(high_ready, turns + DK * b + k + 1)
                    dve.tensor_tensor(xnT[1][:, k, b * SEQ:(b + 1) * SEQ], turned[(DK * b + k) % 4][:, :],
                                      f32(xnT[0][:, k, b * SEQ:(b + 1) * SEQ]),
                                      ALU.subtract).then_inc(low_ready, 1)

            statistics(0)
            statistics(1)
            scales(0)
            statistics(2)
            scales(1)
            statistics(3)
            scales(2)
            low_parts(0)
            scales(3)
            for b in range(1, BATCH):
                low_parts(b)

        @block.scalar
        def _(act):
            def root(b):
                cols = slice(b * BT, (b + 1) * BT)
                act.wait_ge(var_ready, batches + b + 1)
                act.activation(std[:, cols], std[:, cols], ACT.Sqrt).then_inc(std_ready, 1)

            def normalize(b):
                act.wait_ge(scale_ready, batches + b + 1)
                if b >= places:
                    act.wait_ge(turned_ready, turns + DK * (b - places + 1))
                for t in range(BT):
                    i = b * BT + t
                    last = act.activation(xn[:, b % places, t, :], x_sb[:, i, :], ACT.Identity, bias=offset[:, i:i + 1],
                                          scale=rstd[:, i:i + 1])
                last.then_inc(xn_ready, 1)

            def high_parts(b):
                for n in range(DK * b, DK * (b + 1)):
                    act.wait_ge(turned_ready, turns + n + 1)
                    act.copy(xnT[0][:, n % DK, b * SEQ:(b + 1) * SEQ], turned[n % 4][:, :]).then_inc(high_ready, 1)

            root(0)
            root(1)
            normalize(0)
            root(2)
            normalize(1)
            root(3)
            normalize(2)
            high_parts(0)
            normalize(3)
            for b in range(1, BATCH):
                high_parts(b)

        @block.tensor
        def _(pe):
            for n in range(DK * BATCH):
                b, k = divmod(n, DK)
                pe.wait_ge(xn_ready, batches + b + 1)
                if n >= 4:
                    pe.wait_ge(low_ready, turns + n - 3)
                for t in range(BT):
                    last = pe.transpose(turned[n % 4][:, t * P:(t + 1) * P],
                                        xn[:, b % places, t, k * P:(k + 1) * P], ident[:, :])
                last.then_inc(turned_ready, 1)


H0, DH0 = 16, 128
PAIRS = H0 // 2
UNITS = 2 * BATCH
CH = H0 * DH0 // P
QTOK = SEQ // CH
SCALE0 = float(np.float32(1.0) / np.sqrt(np.float32(DH0)))


def step_jobs(last):
    jobs = {}
    for slot in range(1, UNITS + 1):
        if slot % 2 == 0:
            keys, values = (slot // 2 + 1) % BATCH, slot // 2 % BATCH
            make_keys, make_values = not (last and slot >= UNITS - 2), not (last and slot == UNITS)
            jobs[slot] = [[("V", values, 1)] * make_values, [("K", keys, 0)] * make_keys, [], [("K", keys, 1)] * make_keys]
        else:
            done = (slot - 3) // 2 % BATCH
            output = [("O", done, 0), ("O", done, 1)]
            values = [("V", (slot // 2 + 1) % BATCH, 0)]
            if slot < UNITS - 1:
                jobs[slot] = [output, values, [], []]
            elif last:
                jobs[slot] = [output, [], [], []]
            else:
                q = [("Q", c, None) for c in range(CH // 2)]
                jobs[slot] = [[output[0], q[0], output[1]], q[1:4], q[4:6], q[6:] + values]
    return jobs


JOBS = {last: step_jobs(last) for last in (False, True)}
PROLOGUE_JOBS = [("K", 0, 0), ("K", 0, 1), ("V", 0, 0), ("V", 0, 1)] + \
    [("Q", c, None) for c in range(CH // 2)] + [("K", 1, 0), ("K", 1, 1)]
STEP_JOBS = sum(len(part) for parts in JOBS[False].values() for part in parts)
LAST_JOBS = sum(len(part) for parts in JOBS[True].values() for part in parts)
STEP_SPLIT_JOBS = sum(job[0] != "O" for parts in JOBS[False].values() for part in parts for job in part)
LATE_JOBS = 2


def job_numbers(last):
    n = s = 0
    numbered = {}
    for slot in range(1, UNITS + 1):
        for part in range(BT):
            rows = []
            for job in JOBS[last][slot][part]:
                rows.append((job, n, s))
                n += 1
                s += job[0] != "O"
            numbered[slot, part] = rows
    return numbered


NUMBERED = {last: job_numbers(last) for last in (False, True)}


def index_of(kind, *where):
    return next(n for rows in NUMBERED[False].values() for job, n, _ in rows if job == (kind, *where))


class Attention0Loads:

    def __init__(self, m):
        self.probs = [m.sb(f"probs{i}", [P, CAUSAL]) for i in range(2)]
        spare = m.sb("wq_raw", [P, 2, DK * SEQ])
        self.wq_raw = [t.rearrange("p (k n) -> p k n", k=DK) for t in
                       (self.probs[0][:, 0:DK * SEQ], self.probs[1][:, 0:DK * SEQ], spare[:, 0, :], spare[:, 1, :])]
        self.w_raw = m.sb("w_raw", [P, 3, 2, 2 * DH0])
        self.bias_rows = m.sb("bias_rows", [3 * H0, P])
        self.bo_all = m.sb("bo_all", [P, DM])
        self.wq_loaded = [m.sem(f"wq_loaded{c}") for c in range(H0 * DH0 // SEQ)]
        self.bias_loaded, self.weights_loaded = m.sem("bias_loaded"), m.sem("weights_loaded")

    def pair_weights(self, sp, Wk, Wv, Wo, p):
        for i, w in enumerate((Wk, Wv)):
            sp.dma_start(self.w_raw[:, i, :, :], w.rearrange("(k p) n -> p k n", p=P)[:, :, bass.ds(p * 2 * DH0, 2 * DH0)]).then_inc(self.weights_loaded, 16)
        sp.dma_start(self.w_raw[:, 2, :, :], Wo.rearrange("(h p) n -> p h n", p=P)[:, bass.ds(p * 2, 2), :]).then_inc(self.weights_loaded, 16)

    def start(self, sp, Wq, bq, Wk, bk, Wv, bv, Wo, bo):
        self.pair_weights(sp, Wk, Wv, Wo, 0)
        for i, b in enumerate((bq, bk, bv)):
            sp.dma_start(self.bias_rows[i * H0:(i + 1) * H0, :], b.rearrange("(h p) -> h p", p=P)).then_inc(self.bias_loaded, 16)
        sp.dma_start(self.bo_all[:, :], bo.rearrange("(a d) -> a d", a=1).to_broadcast([P, DM])).then_inc(self.bias_loaded, 16)
        for c, loaded in enumerate(self.wq_loaded):
            cols = slice(c * SEQ, (c + 1) * SEQ)
            sp.dma_start(self.wq_raw[c], Wq.rearrange("(k p) n -> p k n", p=P)[:, :, cols]).then_inc(loaded, 16)


def attention0_phase(nc, loads, x_sb, xnT, ident, ident_bf, causal_bf, Wk, Wv, Wo):
    with ExitStack() as ctx:
        m = Memory(nc, ctx, "a0")
        wq = m.pair("wq", [P, DK, H0 * DH0])
        w_raw, bias_rows, bo_all, probs = loads.w_raw, loads.bias_rows, loads.bo_all, loads.probs
        wk = m.pair("wk", [P, DK, 2 * DH0])
        wv = m.pair("wv", [P, DK, 2 * DH0])
        wo = m.pair("wo", [P, 2, DM])
        bias_all = m.sb("bias_all", [P, 3, H0])
        bias_pair = m.sb("bias_pair", [P, 2, 2])
        qT = m.pair("qT", [P, BATCH * 2 * SEQ])
        kT = [m.pair(f"kT{i}", [P, 2 * SEQ]) for i in range(2)]
        vv = [m.pair(f"v{i}", [P, BT * 2 * DH0]) for i in range(2)]
        pT = m.pair("pT", [P, CAUSAL])
        oT = m.pair("oT", [P, 2, SEQ])
        ones = m.sb("ones", [P, 1])
        peak = m.sb("peak", [P, 2, BT])
        shift = m.sb("shift", [P, 2, BT])
        total = m.sb("total", [P, 2, BT])
        inverse = m.sb("inverse", [P, 2, BT])

        score_bank = [m.ps(f"score{i}") for i in range(3)]
        turn_bank = [m.ps(f"turn{i}") for i in range(2)]
        out_bank = m.ps("out")
        proj_bank = [m.ps(f"proj{i}") for i in range(2)]

        wq_loaded, bias_loaded, weights_loaded = loads.wq_loaded, loads.bias_loaded, loads.weights_loaded
        wq_high, wq_split = m.sem("wq_high"), m.sem("wq_split")
        bias_done, bo_added = m.sem("bias_done"), m.sem("bo_added")
        ones_ready = m.sem("ones_ready")
        raw_high, bias_turned = m.sem("raw_high"), m.sem("bias_turned")
        wk_split, wv_split, wo_split = m.sem("wk_split"), m.sem("wv_split"), m.sem("wo_split")
        bk_staged, bv_staged = m.sem("bk_staged"), m.sem("bv_staged")
        proj_ready, proj_high, proj_read = m.sem("proj_ready"), m.sem("proj_high"), m.sem("proj_read")
        scores_ready, peaks, shift_ready = m.sem("scores_ready"), m.sem("peaks"), m.sem("shift_ready")
        exp_done, inverse_ready, probs_ready = m.sem("exp_done"), m.sem("inverse_ready"), m.sem("probs_ready")
        turn_ready, turn_high, turn_read = m.sem("turn_ready"), m.sem("turn_high"), m.sem("turn_read")
        out_ready, out_high, out_read = m.sem("out_ready"), m.sem("out_high"), m.sem("out_read")

        SCORE_TILES = [[(0, 0), (2, P)], [(1, 0)], [(3, 0)]]
        STAT = {0: 0, 2: 1, 1: 2, 3: 3}
        STATS_OF_BANK = [(0, 2), (2, 3), (3, 4)]
        TURN_TILES = [[0], [1], [2, 3]]

        block = ctx.enter_context(nc.Block())

        def job_at(p, n):
            return len(PROLOGUE_JOBS) - LATE_JOBS + STEP_JOBS * p + n

        def split_at(p, n):
            return len(PROLOGUE_JOBS) + STEP_SPLIT_JOBS * p + n

        def bank_of(n):
            return proj_bank[n % 2]

        assert len(PROLOGUE_JOBS) % 2 == 0 and STEP_JOBS % 2 == 0

        @block.sync
        def _(sp):
            with sp.Fori(1, PAIRS) as p:
                sp.wait_ge(wo_split, p)
                loads.pair_weights(sp, Wk, Wv, Wo, p)

        @block.gpsimd
        def _(pool):
            def split_weights(i, pair, count, done):
                raw = w_raw[:, i, :, :].rearrange("p a n -> p (a n)")
                pool.tensor_tensor(pair[0][:, :, :].rearrange("p a n -> p (a n)"), raw, ones[:, 0:1].to_broadcast([P, 4 * DH0]),
                                   ALU.mult).then_inc(raw_high, 1)
                pool.wait_ge(raw_high, count + 1)
                pool.tensor_tensor(pair[1][:, :, :], w_raw[:, i, :, :], f32(pair[0][:, :, :]), ALU.subtract).then_inc(done, 1)

            def normalize(p, u):
                pool.wait_ge(inverse_ready, UNITS * p + u + 1)
                for i in range(BT):
                    rows = probs[u % 2][:, TRI[i]:TRI[i] + (i + 1) * P]
                    by = inverse[:, u % 2, STAT[i]:STAT[i] + 1]
                    if i == 0:
                        last = pool.tensor_tensor(rows, rows, by.to_broadcast([P, P]), ALU.mult)
                    else:
                        last = pool.tensor_scalar(rows, rows, by, 1.0, ALU.mult, ALU.mult)
                last.then_inc(probs_ready, 1)

            def step(p, last):
                for u in range(1, UNITS + 1):
                    if u == UNITS and last:
                        break
                    normalize(p, u)
                    if u == 1:
                        if not isinstance(p, int) or p > 0:
                            pool.wait_ge(proj_ready, job_at(p, LATE_JOBS))
                        split_weights(2, wo, 3 * p + 2, wo_split)
                    if last:
                        continue
                    if u == 4:
                        pool.wait_ge(weights_loaded, 16 * 3 * (p + 2))
                        pool.wait_ge(proj_ready, job_at(p, index_of("K", 3, 1)) + 1)
                        split_weights(0, wk, 3 * p + 3, wk_split)
                    if u == 6:
                        pool.wait_ge(proj_ready, job_at(p, index_of("V", 3, 1)) + 1)
                        split_weights(1, wv, 3 * p + 4, wv_split)

            pool.memset(ones[:, :], 1.0).then_inc(ones_ready, 1)
            pool.wait_ge(ones_ready, 1)
            pool.wait_ge(weights_loaded, 16 * 3)
            split_weights(0, wk, 0, wk_split)
            split_weights(1, wv, 1, wv_split)
            pool.wait_ge(bias_loaded, 16 * 4)
            pool.tensor_tensor(x_sb[:, :, :], x_sb[:, :, :], bo_all[:, :].rearrange("p (a d) -> p a d", a=1).to_broadcast([P, TILES, DM]),
                               ALU.add).then_inc(bo_added, 1)
            normalize(0, 0)
            step(0, False)
            with pool.Fori(1, PAIRS - 1) as p:
                step(p, False)
            step(PAIRS - 1, True)

        @block.tensor
        def _(pe):
            def project(job, p, n, p_of_data):
                kind, a, b = job
                bank = bank_of(n)
                if kind == "K":
                    for k in range(DK):
                        last = split_matmul(pe, bank[:, :], both(wk, slice(None), k, slice(b * DH0, (b + 1) * DH0)),
                                            both(xnT, slice(None), k, slice(a * SEQ, (a + 1) * SEQ)), k == 0, k == DK - 1)
                elif kind == "V":
                    for t in (2 * b, 2 * b + 1):
                        at = a * SEQ + t * P
                        for k in range(DK):
                            last = split_matmul(pe, bank[:, t % 2 * 256:t % 2 * 256 + 256],
                                                both(xnT, slice(None), k, slice(at, at + P)),
                                                both(wv, slice(None), k), k == 0, k == DK - 1)
                elif kind == "Q":
                    for c in (2 * a, 2 * a + 1):
                        for k in range(DK):
                            tokens = tuple(x[:, k, :].rearrange("p (b t) -> p b t", b=BATCH)[:, :, bass.ds(p_of_data * 2 * QTOK, 2 * QTOK)] for x in xnT)
                            out = bank[:, c % 2 * 256:c % 2 * 256 + 256].rearrange("p (b t) -> p b t", b=BATCH)
                            last = split_matmul(pe, out, both(wq, slice(None), k, slice(c * P, (c + 1) * P)),
                                                tokens, k == 0, k == DK - 1)
                else:
                    for t in (2 * b, 2 * b + 1):
                        for j in range(2):
                            last = split_matmul(pe, bank[:, t % 2 * 256:t % 2 * 256 + 256],
                                                both(oT, slice(None), j, slice(t * P, (t + 1) * P)),
                                                both(wo, slice(None), j), j == 0, j == 1)
                last.then_inc(proj_ready, 1)

            def jobs(p, slot, part, last):
                for job, n, _ in NUMBERED[last][slot, part]:
                    if isinstance(p, int) and p == 0 and n < LATE_JOBS:
                        continue
                    if slot == UNITS - 1 and job[0] == "V":
                        pe.wait_ge(wv_split, p + 2)
                    pe.wait_ge(proj_read, job_at(p, n) - 1)
                    project(job, p, n, p + 1)

            def scores(u, bank):
                b, j = divmod(u % UNITS, 2)
                for i, col in SCORE_TILES[bank]:
                    out = score_bank[bank][:, col:col + (i + 1) * P]
                    queries = both(qT, slice(None), slice((2 * b + j) * SEQ + i * P, (2 * b + j) * SEQ + (i + 1) * P))
                    split_matmul(pe, out, queries, both(kT[b % 2], slice(None), slice(j * SEQ, j * SEQ + (i + 1) * P)), True, False)
                    last = pe.matmul(out[:, i * P:], ident_bf[:, :], causal_bf[:, :], start=False, stop=True)
                last.then_inc(scores_ready, 1)

            def turn(u, group):
                col = 0
                for k in TURN_TILES[group]:
                    for i in range(k, BT):
                        last = pe.transpose(turn_bank[group % 2][:, col:col + P],
                                            probs[u % 2][:, TRI[i] + k * P:TRI[i] + (k + 1) * P], ident[:, :])
                        col += P
                last.then_inc(turn_ready, 1)

            def weigh(u, k):
                b, j = divmod(u, 2)
                at = k * 2 * DH0 + j * DH0
                return split_matmul(pe, out_bank[:, k * P:], both(vv[b % 2], slice(None), slice(at, at + DH0)),
                                    both(pT, slice(None), slice(KEY_AT[k], KEY_AT[k] + (BT - k) * P)), k == 0, k == BT - 1)

            def slot(p, u, last=False):
                g = UNITS * p + u
                score = not (last and u == UNITS)
                pe.wait_ge(probs_ready, g)
                pe.wait_ge(turn_read, 3 * g - 3)
                turn(u - 1, 0)
                if score:
                    pe.wait_ge(exp_done, 3 * g - 2)
                    if u == 2:
                        pe.wait_ge(proj_read, job_at(p, LATE_JOBS))
                    elif u % 2 == 0:
                        made = index_of("Q", CH // 2 - 1, None) if u == UNITS else index_of("K", u // 2, 1)
                        pe.wait_ge(proj_read, job_at(p, made) + 1)
                    scores(u, 0)
                turn(u - 1, 1)
                if score:
                    pe.wait_ge(exp_done, 3 * g - 1)
                    scores(u, 1)
                    pe.wait_ge(exp_done, 3 * g)
                    scores(u, 2)
                pe.wait_ge(turn_read, 3 * g - 2)
                pe.wait_ge(out_read, g - 1)
                if u == 1:
                    pe.wait_ge(proj_read, job_at(p, 0))
                elif u % 2:
                    pe.wait_ge(proj_read, job_at(p, index_of("V", u // 2, 1)) + 1)
                weigh(u - 1, 0)
                turn(u - 1, 2)
                jobs(p, u, 0, last)
                pe.wait_ge(turn_read, 3 * g - 1)
                weigh(u - 1, 1)
                jobs(p, u, 1, last)
                pe.wait_ge(turn_read, 3 * g)
                weigh(u - 1, 2)
                jobs(p, u, 2, last)
                weigh(u - 1, 3).then_inc(out_ready, 1)
                jobs(p, u, 3, last)

            def step(p, last=False):
                for u in range(1, UNITS + 1):
                    if u == 3:
                        pe.wait_ge(wo_split, p + 1)
                    if u == UNITS - 2 and not last:
                        pe.wait_ge(wk_split, p + 2)
                    slot(p, u, last)

            pe.wait_ge(bias_loaded, 16 * 4)
            pe.transpose(turn_bank[0][:, 0:3 * H0], bias_rows[:, :], ident[0:3 * H0, 0:3 * H0]).then_inc(bias_turned, 1)
            pe.wait_ge(wk_split, 1)
            for n, job in enumerate(PROLOGUE_JOBS):
                if job[0] == "V":
                    pe.wait_ge(wv_split, 1)
                if job[0] == "Q":
                    pe.wait_ge(wq_split, 2 * job[1] * P // SEQ + 1)
                if n >= 2:
                    pe.wait_ge(proj_read, n - 1)
                project(job, 0, n, 0)
                if n == len(PROLOGUE_JOBS) - 3:
                    pe.wait_ge(proj_read, n + 1)
                    for bank in range(3):
                        scores(0, bank)
            step(0)
            with pe.Fori(1, PAIRS - 1) as p:
                step(p)
            step(PAIRS - 1, True)
            pe.wait_ge(out_read, UNITS * PAIRS)
            for half in range(2):
                pe.wait_ge(proj_read, job_at(PAIRS - 1, LAST_JOBS + half) - 1)
                project(("O", BATCH - 1, half), PAIRS - 1, LAST_JOBS + half, None)

        def evacuation(job, n):
            kind, a, b = job
            bank = bank_of(n)
            if kind == "K":
                return [(both(kT[a % 2], slice(None), slice(b * SEQ, (b + 1) * SEQ)), bank[:, :], bias_pair[:, 0, b:b + 1])]
            if kind == "V":
                return [(both(vv[a % 2], slice(None), slice(b * 512, (b + 1) * 512)), bank[:, :], None)]
            pieces = []
            for c in (2 * a, 2 * a + 1):
                out = tuple(x[:, :].rearrange("p (t c) -> p t c", c=CH)[:, :, c] for x in qT)
                pieces.append((out, bank[:, c % 2 * 256:c % 2 * 256 + 256], bias_all[:, 0, c:c + 1]))
            return pieces

        @block.scalar
        def _(act):
            def high(p, job, n, s):
                act.wait_ge(proj_ready, n_of(p, n) + 1)
                for out, src, bias in evacuation(job, n):
                    last = act.copy(out[0], src) if bias is None else act.activation(out[0], src, ACT.Identity, bias=bias)
                last.then_inc(proj_high, 1)

            def n_of(p, n):
                return n if p is None else job_at(p, n)

            def jobs(p, slot, part, last):
                for job, n, s in NUMBERED[last][slot, part]:
                    if job[0] != "O":
                        high(p, job, n, s)

            def exps(p, u, bank):
                g = UNITS * p + u
                act.wait_ge(shift_ready, 3 * g + bank + 1)
                for i, col in SCORE_TILES[bank]:
                    c = STAT[i]
                    last = act.activation(probs[u % 2][:, TRI[i]:TRI[i] + (i + 1) * P], score_bank[bank][:, col:col + (i + 1) * P],
                                          ACT.Exp, bias=shift[:, u % 2, c:c + 1], scale=SCALE0, accum_out=total[:, u % 2, c:c + 1])
                last.then_inc(exp_done, 1)

            def turned(p, u, group):
                g = UNITS * p + u
                act.wait_ge(turn_ready, 3 * g - 2 + group)
                at = KEY_AT[TURN_TILES[group][0]]
                width = sum((BT - k) * P for k in TURN_TILES[group])
                act.copy(pT[0][:, at:at + width], turn_bank[group % 2][:, 0:width]).then_inc(turn_high, 1)

            def slot(p, u, last=False):
                g = UNITS * p + u
                score = not (last and u == UNITS)
                turned(p, u, 0)
                turned(p, u, 1)
                if score:
                    exps(p, u, 0)
                    exps(p, u, 1)
                turned(p, u, 2)
                if score:
                    exps(p, u, 2)
                for part in range(3):
                    jobs(p, u, part, last)
                if u == 1:
                    act.wait_ge(bv_staged, p + 1)
                act.wait_ge(out_ready, g)
                j = (u - 1) % 2
                act.activation(oT[0][:, j, :], out_bank[:, :], ACT.Identity, bias=bias_pair[:, 1, j:j + 1]).then_inc(out_high, 1)
                jobs(p, u, 3, last)

            def step(p, last=False):
                for u in range(1, UNITS + 1):
                    if u == UNITS - 2 and not last:
                        act.wait_ge(bk_staged, p + 2)
                    slot(p, u, last)

            act.wait_ge(bk_staged, 1)
            for n, job in enumerate(PROLOGUE_JOBS):
                if n < len(wq_loaded):
                    cols = slice(n * SEQ, (n + 1) * SEQ)
                    act.wait_ge(wq_loaded[n], 16)
                    act.copy(wq[0][:, :, cols], loads.wq_raw[n]).then_inc(wq_high, 1)
                high(None, job, n, n)
                if n == len(PROLOGUE_JOBS) - 3:
                    for bank in range(3):
                        exps(0, 0, bank)
            step(0)
            with act.Fori(1, PAIRS - 1) as p:
                step(p)
            step(PAIRS - 1, True)

        @block.vector
        def _(dve):
            def low(p, job, n, s):
                dve.wait_ge(proj_high, (s if p is None else split_at(p, s)) + 1)
                for out, src, bias in evacuation(job, n):
                    if bias is None:
                        last = dve.tensor_tensor(out[1], src, f32(out[0]), ALU.subtract)
                    else:
                        last = dve.scalar_tensor_tensor(out[1], src, bias, f32(out[0]), ALU.add, ALU.subtract)
                last.then_inc(proj_read, 1)

            def jobs(p, slot, part, last):
                for job, n, s in NUMBERED[last][slot, part]:
                    if isinstance(p, int) and p == 0 and n < LATE_JOBS:
                        continue
                    if job[0] == "O":
                        add_output(p, job, n)
                    else:
                        low(p, job, n, s)

            def add_output(p, job, n):
                _, b, half = job
                dve.wait_ge(proj_ready, job_at(p, n) + 1)
                t = b * BT + 2 * half
                rows = x_sb[:, t:t + 2, :].rearrange("p t d -> p (t d)")
                dve.tensor_tensor(rows, bank_of(n)[:, :], rows, ALU.add).then_inc(proj_read, 1)

            def peak_of(p, u, bank):
                g = UNITS * p + u
                dve.wait_ge(scores_ready, 3 * g + bank + 1)
                for i, col in SCORE_TILES[bank]:
                    c = STAT[i]
                    last = dve.reduce_max(peak[:, u % 2, c:c + 1], score_bank[bank][:, col:col + (i + 1) * P], AX.X)
                last.then_inc(peaks, 1)
                dve.wait_ge(peaks, 3 * g + bank + 1)
                lo, hi = STATS_OF_BANK[bank]
                dve.tensor_scalar(shift[:, u % 2, lo:hi], peak[:, u % 2, lo:hi], -SCALE0, None, ALU.mult).then_inc(shift_ready, 1)

            def invert(p, u):
                g = UNITS * p + u
                dve.wait_ge(exp_done, 3 * g + 3)
                dve.reciprocal(inverse[:, u % 2, :], total[:, u % 2, :]).then_inc(inverse_ready, 1)

            def turned(p, u, group):
                g = UNITS * p + u
                dve.wait_ge(turn_high, 3 * g - 2 + group)
                at = KEY_AT[TURN_TILES[group][0]]
                width = sum((BT - k) * P for k in TURN_TILES[group])
                dve.tensor_tensor(pT[1][:, at:at + width], turn_bank[group % 2][:, 0:width],
                                  f32(pT[0][:, at:at + width]), ALU.subtract).then_inc(turn_read, 1)

            def slot(p, u, last=False):
                g = UNITS * p + u
                score = not (last and u == UNITS)
                turned(p, u, 0)
                if score:
                    peak_of(p, u, 0)
                turned(p, u, 1)
                if score:
                    peak_of(p, u, 1)
                    peak_of(p, u, 2)
                turned(p, u, 2)
                if u == 1:
                    dve.tensor_copy(bias_pair[:, 1, :], bias_all[:, 2, bass.ds(p * 2, 2)]).then_inc(bv_staged, 1)
                    dve.wait_ge(bv_staged, p + 1)
                if score:
                    invert(p, u)
                for part in range(3):
                    jobs(p, u, part, last)
                dve.wait_ge(out_high, g)
                j = (u - 1) % 2
                dve.scalar_tensor_tensor(oT[1][:, j, :], out_bank[:, :], bias_pair[:, 1, j:j + 1], f32(oT[0][:, j, :]),
                                         ALU.add, ALU.subtract).then_inc(out_read, 1)
                jobs(p, u, 3, last)

            def step(p, last=False):
                for u in range(1, UNITS + 1):
                    if u == UNITS - 2 and not last:
                        dve.tensor_copy(bias_pair[:, 0, :], bias_all[:, 1, bass.ds(p * 2 + 2, 2)]).then_inc(bk_staged, 1)
                        dve.wait_ge(bk_staged, p + 2)
                    slot(p, u, last)

            dve.wait_ge(bias_turned, 1)
            dve.tensor_copy(bias_all[:, :, :], turn_bank[0][:, 0:3 * H0]).then_inc(bias_done, 1)
            dve.wait_ge(bias_done, 1)
            dve.tensor_copy(bias_pair[:, 0, :], bias_all[:, 1, 0:2]).then_inc(bk_staged, 1)
            dve.wait_ge(bk_staged, 1)
            for n, job in enumerate(PROLOGUE_JOBS):
                if n < len(wq_loaded):
                    cols = slice(n * SEQ, (n + 1) * SEQ)
                    dve.wait_ge(wq_high, n + 1)
                    dve.tensor_tensor(wq[1][:, :, cols], loads.wq_raw[n], f32(wq[0][:, :, cols]), ALU.subtract).then_inc(wq_split, 1)
                low(None, job, n, n)
                if n == len(PROLOGUE_JOBS) - 3:
                    for bank in range(3):
                        peak_of(0, 0, bank)
                    invert(0, 0)
            dve.wait_ge(bo_added, 1)
            step(0)
            with dve.Fori(1, PAIRS - 1) as p:
                step(p)
            step(PAIRS - 1, True)
            for half in range(2):
                add_output(PAIRS - 1, ("O", BATCH - 1, half), LAST_JOBS + half)

E0, DF0 = 8, 256
FK0 = DF0 // P
CHUNKS = BATCH


def moe0_phase(nc, x_sb, xnT, ident, w_router, w_fc, w_proj):
    with ExitStack() as ctx:
        m = Memory(nc, ctx, "m0")
        router_raw = m.sb("router_raw", [P, DK, E0])
        router = m.pair("router", [P, DK, E0])
        logits_T = m.sb("logits_T", [E0, TOKENS])
        logits = m.sb("logits", [P, TILES, E0])
        top = m.sb("top", [P, TILES, 8])
        top_at = m.sb("top_at", [P, TILES, 8], mybir.dt.uint32)
        top_id = m.sb("top_id", [P, TILES, 8])
        expert_id = m.sb("expert_id", [P, E0])
        gap = m.sb("gap", [P, TILES])
        share = m.sb("share", [P, 2, TILES])
        hit = m.sb("hit", [P, 2, TILES * E0])
        combine = m.sb("combine", [P, TILES, E0])
        ones = m.sb("ones", [P, 1])
        w_raw = [m.sb(f"w_raw{i}", [P, 2, 2 * DM]) for i in range(2)]
        fc = [m.pair(f"fc{i}", [P, DK, DF0]) for i in range(2)]
        proj = [m.pair(f"proj{i}", [P, FK0, DM]) for i in range(2)]
        relu = m.sb("relu", [P, 2, SEQ])
        square = m.sb("square", [P, 2, SEQ])
        hT = [m.pair(f"hT{i}", [P, FK0, SEQ]) for i in range(2)]
        up_bank = [m.ps(f"up{i}") for i in range(4)]
        down_bank = [m.ps(f"down{i}") for i in range(4)]

        router_loaded, router_high, router_split = m.sem("router_loaded"), m.sem("router_high"), m.sem("router_split")
        logits_ready, chain, ids_ready, gap_ready, exp_ready = (m.sem(n) for n in ("logits_ready", "chain", "ids_ready", "gap_ready", "exp_ready"))
        logits_made, logits_copied = m.sem("logits_made"), m.sem("logits_copied")
        combine_ready = m.sem("combine_ready")
        raw_loaded = [m.sem(f"raw_loaded{i}") for i in range(2)]
        raw_high = m.sem("raw_high")
        split_done = [m.sem(f"split_done{i}") for i in range(2)]
        up_ready, relu_ready, square_ready, high_ready, low_ready = (m.sem(n) for n in ("up_ready", "relu_ready", "square_ready", "high_ready", "low_ready"))
        down_ready, down_read = m.sem("down_ready"), m.sem("down_read")
        block = ctx.enter_context(nc.Block())
        STEPS = E0 // 2
        PER_STEP = 2 * CHUNKS

        def fc_of(e):
            return w_fc[e].rearrange("(k p) n -> p k n", p=P)

        @block.sync
        def _(sp):
            sp.dma_start(router_raw[:, :, :], w_router.rearrange("(k p) e -> p k e", p=P)).then_inc(router_loaded, 16)

            def load(e, i, done):
                if not isinstance(done, int) or done > 0:
                    sp.wait_ge(split_done[i], done)
                for j, w in enumerate((w_fc, w_proj)):
                    src = w.rearrange("e (k p) n -> p e k n", p=P)[:, bass.ds(e, 1), :, :]
                    sp.dma_start(w_raw[i][:, j, :].rearrange("p (a k n) -> p a k n", a=1, k=DK), src).then_inc(raw_loaded[i], 16)

            load(0, 0, 0)
            load(1, 1, 0)
            with sp.Fori(1, STEPS) as p:
                load(2 * p, 0, p)
                load(2 * p + 1, 1, p)

        @block.gpsimd
        def _(pool):
            pool.memset(ones[:, :], 1.0).then_inc(raw_high, 1)
            pool.iota(expert_id[:, :], pattern=[[1, E0]], base=0, channel_multiplier=0,
                      allow_small_or_imprecise_dtypes=True).then_inc(ids_ready, 1)
            pool.wait_ge(raw_high, 1)

            def split_weights(i, p, count):
                pool.wait_ge(raw_loaded[i], 32 * (p + 1))
                for j, pair in enumerate((fc[i], proj[i])):
                    raw = w_raw[i][:, j, :]
                    high, low = (t[:, :, :].rearrange("p k n -> p (k n)") for t in pair)
                    pool.tensor_tensor(high, raw, ones[:, 0:1].to_broadcast([P, 2 * DM]), ALU.mult).then_inc(raw_high, 1)
                    pool.wait_ge(raw_high, 2 * count + j + 2)
                    last = pool.tensor_tensor(low, raw, f32(high), ALU.subtract)
                last.then_inc(split_done[i], 1)

            def step(p, last=False):
                for c in range(PER_STEP):
                    n = PER_STEP * p + c
                    for i in range(FK0):
                        pool.wait_ge(high_ready, FK0 * n + i + 1)
                        pool.tensor_tensor(hT[c % 2][1][:, i, :], square[:, i, :], f32(hT[c % 2][0][:, i, :]),
                                           ALU.subtract).then_inc(low_ready, 1)
                    if c == 1 and not (isinstance(p, int) and p == 0):
                        pool.wait_ge(down_ready, 2 * PER_STEP * p)
                        split_weights(1, p, 2 * p + 1)
                    if c == CHUNKS + 1 and not last:
                        pool.wait_ge(down_ready, 2 * (PER_STEP * p + CHUNKS))
                        split_weights(0, p + 1, 2 * p + 2)

            split_weights(0, 0, 0)
            split_weights(1, 0, 1)
            step(0)
            with pool.Fori(1, STEPS - 1) as p:
                step(p)
            step(STEPS - 1, True)

        @block.tensor
        def _(pe):
            pe.wait_ge(router_split, 1)
            for c in range(CHUNKS):
                for k in range(DK):
                    last = split_matmul(pe, up_bank[c][0:E0, :], both(router, slice(None), k),
                                        both(xnT, slice(None), k, slice(c * SEQ, (c + 1) * SEQ)), k == 0, k == DK - 1)
                last.then_inc(logits_made, 1)
            for t in range(TILES):
                if t % BT == 0:
                    pe.wait_ge(logits_copied, t // BT + 1)
                last = pe.transpose(down_bank[0][:, t * E0:(t + 1) * E0], logits_T[:, t * P:(t + 1) * P], ident[0:E0, 0:E0])
            last.then_inc(logits_ready, 1)

            def up(p, c):
                n = PER_STEP * p + c
                for i in range(FK0):
                    at = 2 * (c % 2) + i
                    if not isinstance(n, int) or n >= 2:
                        pe.wait_ge(square_ready, FK0 * (n - 2) + i + 1)
                    tokens = c % CHUNKS
                    for k in range(DK):
                        last = split_matmul(pe, up_bank[at][:, :], both(fc[c // CHUNKS], slice(None), k, slice(i * P, (i + 1) * P)),
                                            both(xnT, slice(None), k, slice(tokens * SEQ, (tokens + 1) * SEQ)), k == 0, k == DK - 1)
                    last.then_inc(up_ready, 1)

            def down(p, c):
                n = PER_STEP * p + c
                pe.wait_ge(low_ready, FK0 * (n + 1))
                for half in range(2):
                    if not isinstance(n, int) or n >= 2:
                        pe.wait_ge(down_read, 2 * (n - 2) + half + 1)
                    elif n == 0:
                        pe.wait_ge(combine_ready, 1)
                    for t in (2 * half, 2 * half + 1):
                        for i in range(FK0):
                            last = split_matmul(pe, down_bank[2 * (c % 2) + half][:, t % 2 * DM:(t % 2 + 1) * DM],
                                                both(hT[c % 2], slice(None), i, slice(t * P, (t + 1) * P)),
                                                both(proj[c // CHUNKS], slice(None), i), i == 0, i == FK0 - 1)
                    last.then_inc(down_ready, 1)

            def step(p):
                for c in range(PER_STEP):
                    if c % CHUNKS == 0:
                        pe.wait_ge(split_done[c // CHUNKS], p + 1)
                    up(p, c)
                    if c:
                        down(p, c - 1)
                    elif not isinstance(p, int) or p > 0:
                        down(p - 1, PER_STEP - 1)

            step(0)
            with pe.Fori(1, STEPS) as p:
                step(p)
            down(STEPS - 1, PER_STEP - 1)

        @block.scalar
        def _(act):
            act.wait_ge(router_loaded, 16)
            act.copy(router[0][:, :, :], router_raw[:, :, :]).then_inc(router_high, 1)
            for c in range(CHUNKS):
                act.wait_ge(logits_made, c + 1)
                act.copy(logits_T[:, c * SEQ:(c + 1) * SEQ], up_bank[c][0:E0, :]).then_inc(logits_copied, 1)
            act.wait_ge(gap_ready, 1)
            act.activation(gap[:, :], gap[:, :], ACT.Exp).then_inc(exp_ready, 1)

            def chunk(p, c):
                n = PER_STEP * p + c
                for i in range(FK0):
                    act.wait_ge(up_ready, FK0 * n + i + 1)
                    if not isinstance(n, int) or n >= 1:
                        act.wait_ge(square_ready, FK0 * (n - 1) + i + 1)
                    act.activation(relu[:, i, :], up_bank[2 * (c % 2) + i][:, :], ACT.Relu).then_inc(relu_ready, 1)
                for i in range(FK0):
                    act.wait_ge(square_ready, FK0 * n + i + 1)
                    if not isinstance(n, int) or n >= 2:
                        act.wait_ge(down_ready, 2 * (n - 1))
                    act.copy(hT[c % 2][0][:, i, :], square[:, i, :]).then_inc(high_ready, 1)

            def step(p):
                for c in range(PER_STEP):
                    chunk(p, c)

            step(0)
            with act.Fori(1, STEPS) as p:
                step(p)

        @block.vector
        def _(dve):
            count = [0]

            def mine(instruction):
                count[0] += 1
                instruction.then_inc(chain, 1)
                dve.wait_ge(chain, count[0])

            dve.wait_ge(router_high, 1)
            dve.tensor_tensor(router[1][:, :, :], router_raw[:, :, :], f32(router[0][:, :, :]), ALU.subtract).then_inc(router_split, 1)
            dve.wait_ge(logits_ready, 1)
            mine(dve.tensor_copy(logits[:, :, :].rearrange("p t e -> p (t e)"), down_bank[0][:, 0:TILES * E0]))
            for t in range(TILES):
                last = dve.max(top[:, t, :], logits[:, t, :])
            mine(last)
            for t in range(TILES):
                last = dve.max_index(top_at[:, t, :], top[:, t, :], logits[:, t, :])
            mine(last)
            dve.tensor_tensor(gap[:, :], top[:, :, 1], top[:, :, 0], ALU.subtract).then_inc(gap_ready, 1)
            mine(dve.tensor_copy(top_id[:, :, 0:2], top_at[:, :, 0:2]))
            dve.wait_ge(ids_ready, 1)
            ids = expert_id[:, :].rearrange("p (a e) -> p a e", a=1).to_broadcast([P, TILES, E0])
            hits = [hit[:, j, :].rearrange("p (t e) -> p t e", e=E0) for j in range(2)]
            for j in range(2):
                dve.tensor_tensor(hits[j], ids, top_id[:, :, j:j + 1].to_broadcast([P, TILES, E0]), ALU.is_equal)
            dve.wait_ge(exp_ready, 1)
            mine(dve.tensor_scalar(share[:, 1, :], gap[:, :], 1.0, None, ALU.add))
            mine(dve.reciprocal(share[:, 0, :], share[:, 1, :]))
            mine(dve.tensor_tensor(share[:, 1, :], gap[:, :], share[:, 0, :], ALU.mult))
            for j in range(2):
                last = dve.tensor_tensor(hits[j], hits[j], share[:, j, :].rearrange("p (t a) -> p t a", a=1).to_broadcast([P, TILES, E0]), ALU.mult)
            mine(last)
            dve.tensor_tensor(combine[:, :, :], hits[0], hits[1], ALU.add).then_inc(combine_ready, 1)

            def squares(p, c):
                n = PER_STEP * p + c
                for i in range(FK0):
                    dve.wait_ge(relu_ready, FK0 * n + i + 1)
                    if not isinstance(n, int) or n >= 1:
                        dve.wait_ge(low_ready, FK0 * (n - 1) + i + 1)
                    dve.tensor_tensor(square[:, i, :], up_bank[2 * (c % 2) + i][:, :], relu[:, i, :], ALU.mult).then_inc(square_ready, 1)

            def outputs(p, c):
                n = PER_STEP * p + c
                e = 2 * p + c // CHUNKS
                for half in range(2):
                    dve.wait_ge(down_ready, 2 * n + half + 1)
                    for t in (2 * half, 2 * half + 1):
                        tile = c % CHUNKS * BT + t
                        last = dve.scalar_tensor_tensor(x_sb[:, tile, :], down_bank[2 * (c % 2) + half][:, t % 2 * DM:(t % 2 + 1) * DM],
                                                        combine[:, tile, bass.ds(e, 1)], x_sb[:, tile, :], ALU.mult, ALU.add)
                    last.then_inc(down_read, 1)

            def step(p):
                for c in range(PER_STEP):
                    squares(p, c)
                    if c:
                        outputs(p, c - 1)
                    elif not isinstance(p, int) or p > 0:
                        outputs(p - 1, PER_STEP - 1)

            dve.wait_ge(combine_ready, 1)
            step(0)
            with dve.Fori(1, STEPS) as p:
                step(p)
            outputs(STEPS - 1, PER_STEP - 1)

H1, DH1 = 16, 16
HALF = P // DH1
HALVES = 2 * BATCH
PRODUCTS = [(0, 0), (0, 1), (1, 0), (1, 1), (0, 2), (2, 0), (1, 2), (2, 1)]
LEAD = 4
SCALE1 = 1.0 / float(np.sqrt(np.float32(DH1)))


class Attention1Loads:

    def __init__(self, m):
        self.w_qkv, self.w_out = m.sb("w_qkv", [P, DK, 3 * DM]), m.sb("w_out", [P, 2, DM])
        self.qkv_loaded, self.out_loaded = m.sem("qkv_loaded"), m.sem("out_loaded")

    def start(self, sp, w_qkv, w_out):
        sp.dma_start(self.w_qkv[:, :, :], w_qkv.rearrange("(k p) n -> p k n", p=P)).then_inc(self.qkv_loaded, 16)
        sp.dma_start(self.w_out[:, :, :], w_out.rearrange("(k p) n -> p k n", p=P)).then_inc(self.out_loaded, 16)


class Stacks:

    def __init__(self, m, parts_dram):
        self.parts_dram = parts_dram
        self.qs = m.sb("qs", [P, 2 * HALF * SEQ], BF16)
        self.ks = m.sb("ks", [P, 2 * HALF * SEQ], BF16)
        self.first_loaded = m.sem("first_stacks_loaded")
        self.loaded = m.sem("stacks_loaded")

    def load(self, queue, s, loaded):
        for which, stack in enumerate((self.qs, self.ks)):
            for row, product in enumerate(PRODUCTS):
                src = self.parts_dram[which, product[which]].rearrange("b (f h d) t -> d (b f) h t", f=2, d=DH1)
                out = stack[row * DH1:(row + 1) * DH1, bass.ds((s % 2) * (HALF * SEQ), HALF * SEQ)]
                queue.dma_start(out.rearrange("p (a h t) -> p a h t", a=1, h=HALF), src[:, bass.ds(s, 1), :, :]).then_inc(loaded, 16)


STACK_DMAS = 2 * len(PRODUCTS)


def project1_phase(nc, loads, stacks, xnT, parts_dram, values):
    with ExitStack() as ctx:
        m = Memory(nc, ctx, "p1")
        raw, raw_loaded = loads.w_qkv, loads.qkv_loaded
        w = m.pair("w", [P, DK, 3 * DM])
        parts = m.sb("parts", [P, 4, 3, SEQ], BF16)
        rest = m.sb("rest", [P, 3, SEQ])
        bank = [m.ps(f"bank{i}") for i in range(6)]
        w_high, w_split = m.sem("w_high"), m.sem("w_split")
        proj_ready, first, rest_ready, second, third = (m.sem(n) for n in ("proj_ready", "first", "rest_ready", "second", "third"))
        values_read = m.sem("values_read")
        stored = [m.sem(f"stored{i}") for i in range(4)]
        block = ctx.enter_context(nc.Block())
        PER_BATCH = 6
        QK = [(which, half) for half in range(2) for which in range(2)]

        @block.sync
        def _(sp):
            for n in range(4 * BATCH):
                b, (which, half) = n // 4, QK[n % 4]
                sp.wait_ge(third, n + 1)
                sp.wait_ge(second, n + 1)
                sp.dma_start(parts_dram[which, :, b, half * P:(half + 1) * P, :].rearrange("s r t -> r s t"),
                             parts[:, n % 4, :, :]).then_inc(stored[n % 4], 16)
            for i in range(4):
                sp.wait_ge(stored[i], 16 * BATCH)

        @block.gpsimd
        def _(pool):
            pool.wait_ge(first, 6)
            stacks.load(pool, 0, stacks.first_loaded)

        @block.tensor
        def _(pe):
            pe.wait_ge(w_split, 1)
            for b in range(BATCH):
                for j in range(2):
                    if b:
                        pe.wait_ge(values_read, 2 * b + j - 1)
                    for t in (2 * j, 2 * j + 1):
                        at = b * SEQ + t * P
                        for k in range(DK):
                            last = split_matmul(pe, bank[j][:, t % 2 * DM:(t % 2 + 1) * DM], both(xnT, slice(None), k, slice(at, at + P)),
                                                both(w, slice(None), k, slice(2 * DM, 3 * DM)), k == 0, k == DK - 1)
                    last.then_inc(proj_ready, 1)
                for j, (which, half) in enumerate(QK):
                    if b:
                        pe.wait_ge(rest_ready, 4 * (b - 1) + j + 1)
                    at = which * DM + half * P
                    for k in range(DK):
                        last = split_matmul(pe, bank[2 + j][:, :], both(w, slice(None), k, slice(at, at + P)),
                                            both(xnT, slice(None), k, slice(b * SEQ, (b + 1) * SEQ)), k == 0, k == DK - 1)
                    last.then_inc(proj_ready, 1)

        @block.scalar
        def _(act):
            def second_part(n):
                act.wait_ge(rest_ready, n + 1)
                act.copy(parts[:, n % 4, 1, :], rest[:, n % 3, :]).then_inc(second, 1)

            act.wait_ge(raw_loaded, 16)
            act.copy(w[0][:, :, :], raw[:, :, :]).then_inc(w_high, 1)
            for b in range(BATCH):
                for j in range(2):
                    act.wait_ge(proj_ready, PER_BATCH * b + j + 1)
                    for t in range(2):
                        out = values[:, 2 * b:2 * b + 2, 2 * j + t, :]
                        last = act.copy(out, bank[j][:, t * DM:(t + 1) * DM].rearrange("p (h d) -> p h d", h=2))
                    last.then_inc(values_read, 1)
                for j in range(4):
                    n = 4 * b + j
                    act.wait_ge(proj_ready, PER_BATCH * b + 2 + j + 1)
                    if n >= 4:
                        act.wait_ge(stored[n % 4], 16 * (n // 4))
                    act.copy(parts[:, n % 4, 0, :], bank[2 + j][:, :]).then_inc(first, 1)
                    if n:
                        second_part(n - 1)
            second_part(4 * BATCH - 1)

        @block.vector
        def _(dve):
            dve.wait_ge(w_high, 1)
            dve.tensor_tensor(w[1][:, :, :], raw[:, :, :], f32(w[0][:, :, :]), ALU.subtract).then_inc(w_split, 1)

            def third_part(n):
                dve.wait_ge(second, n + 1)
                dve.tensor_tensor(parts[:, n % 4, 2, :], rest[:, n % 3, :], parts[:, n % 4, 1, :], ALU.subtract).then_inc(third, 1)

            for n in range(4 * BATCH):
                dve.wait_ge(first, n + 1)
                if n >= 3:
                    dve.wait_ge(third, n - 2)
                dve.tensor_tensor(rest[:, n % 3, :], bank[2 + n % 4][:, :], parts[:, n % 4, 0, :], ALU.subtract).then_inc(rest_ready, 1)
                if n:
                    third_part(n - 1)
            third_part(4 * BATCH - 1)


def attention1_phase(nc, loads, stacks, x_sb, values, ident, ident_bf, causal_bf):
    with ExitStack() as ctx:
        m = Memory(nc, ctx, "a1")
        qs, ks, stacks_loaded = stacks.qs, stacks.ks, stacks.loaded
        GAP = BT * P + DH1
        placed = tuple(m.sb(n, [P, HALF * GAP], F32R) for n in ("placed_hi", "placed_lo"))
        w_raw, w_loaded = loads.w_out, loads.out_loaded
        w_pair = m.pair("w", [P, 2, DM])
        probs = [m.sb(f"probs{i}", [P, CAUSAL]) for i in range(4)]
        pT = [m.pair(f"pT{i}", [P, CAUSAL]) for i in range(2)]
        oT = m.pair("oT", [P, SEQ])
        peak = m.sb("peak", [P, 4, BT])
        shift = m.sb("shift", [P, 4, BT])
        total = m.sb("total", [P, 4, BT])
        inverse = m.sb("inverse", [P, 4, BT])
        score_bank = [m.ps(f"score{i}") for i in range(3)]
        turn_bank = [m.ps(f"turn{i}") for i in range(3)]
        out_bank = m.ps("out")
        proj_bank = m.ps("proj")

        w_high, w_split = m.sem("w_high"), m.sem("w_split")
        zeroed, values_placed, placed_high = (m.sem(n) for n in ("zeroed", "values_placed", "placed_high"))
        scores_ready, peaks, shift_ready = m.sem("scores_ready"), m.sem("peaks"), m.sem("shift_ready")
        exp_done, inverse_ready, probs_ready = m.sem("exp_done"), m.sem("inverse_ready"), m.sem("probs_ready")
        turn_ready, turn_high, turn_read = m.sem("turn_ready"), m.sem("turn_high"), m.sem("turn_read")
        weighed = m.sem("weighed")
        out_high, out_read = m.sem("out_high"), m.sem("out_read")
        proj_ready, proj_read = m.sem("proj_ready"), m.sem("proj_read")

        SCORE_TILES = [[(0, 0), (2, P)], [(1, 0)], [(3, 0)]]
        STAT = {0: 0, 2: 1, 1: 2, 3: 3}
        STATS_OF_BANK = [(0, 2), (2, 3), (3, 4)]
        TURN_TILES = [[0], [1], [2, 3]]
        block = ctx.enter_context(nc.Block())

        @block.sync
        def _(sp):
            stacks.load(sp, 1, stacks_loaded)
            with sp.Fori(2, HALVES) as s:
                sp.wait_ge(scores_ready, 3 * HALF * (s - 1))
                sp.wait_ge(stacks_loaded, 16 * STACK_DMAS * s - 16 * STACK_DMAS)
                stacks.load(sp, s, stacks_loaded)

        @block.gpsimd
        def _(pool):
            for t in placed:
                pool.memset(t[:, :].bitcast(F32), 0.0).then_inc(zeroed, 1)

            def normalize(s, u):
                pool.wait_ge(inverse_ready, HALF * s + u + 1)
                for i in range(BT):
                    rows = probs[u % 4][:, TRI[i]:TRI[i] + (i + 1) * P]
                    by = inverse[:, u % 4, STAT[i]:STAT[i] + 1]
                    if i == 0:
                        last = pool.tensor_tensor(rows, rows, by.to_broadcast([P, P]), ALU.mult)
                    else:
                        last = pool.tensor_scalar(rows, rows, by, 1.0, ALU.mult, ALU.mult)
                last.then_inc(probs_ready, 1)

            with pool.Fori(0, HALVES) as s:
                for u in range(HALF):
                    normalize(s, u)

        @block.tensor
        def _(pe):
            def scores(s, u, bank):
                at = ((s + u // HALF) % 2) * (HALF * SEQ) + u % HALF * SEQ
                for i, col in SCORE_TILES[bank]:
                    out = score_bank[bank][:, col:col + (i + 1) * P]
                    pe.matmul(out, qs[:, bass.ds(at + i * P, P)], ks[:, bass.ds(at, (i + 1) * P)], start=True, stop=False)
                    last = pe.matmul(out[:, i * P:], ident_bf[:, :], causal_bf[:, :], start=False, stop=True)
                last.then_inc(scores_ready, 1)

            def turn(v, group):
                col = 0
                for k in TURN_TILES[group]:
                    for i in range(k, BT):
                        last = pe.transpose(turn_bank[group][:, col:col + P],
                                            probs[v % 4][:, TRI[i] + k * P:TRI[i] + (k + 1) * P], ident[:, :])
                        col += P
                last.then_inc(turn_ready, 1)

            def weigh(w, k):
                at = w * BT * P + k * P
                return split_matmul(pe, out_bank[:, k * P:], both(placed, slice(None), slice(at, at + P)),
                                    both(pT[w % 2], slice(None), slice(KEY_AT[k], KEY_AT[k] + (BT - k) * P)),
                                    w == 0 and k == 0, w == HALF - 1 and k == BT - 1)

            def project(s, j):
                for t in (2 * j, 2 * j + 1):
                    last = split_matmul(pe, proj_bank[:, t % 2 * DM:(t % 2 + 1) * DM], both(oT, slice(None), slice(t * P, (t + 1) * P)),
                                        tuple(x[:, bass.ds(s % 2, 1), :].rearrange("p a d -> p (a d)") for x in w_pair), True, True)
                last.then_inc(proj_ready, 1)

            def slot(s, w, last=False):
                v, u = w + 1, w + LEAD
                g = HALF * s + w
                turning, scoring = not (last and v >= HALF), not (last and u >= HALF)
                first = isinstance(s, int) and s == 0
                for bank in range(3):
                    if turning:
                        if bank == 0:
                            pe.wait_ge(probs_ready, g + 2)
                        pe.wait_ge(turn_read, 3 * g + bank + 1)
                        turn(v, bank)
                    if scoring:
                        if bank == 0 and u == HALF:
                            pe.wait_ge(stacks_loaded, 16 * STACK_DMAS * (s + 1))
                        pe.wait_ge(exp_done, 3 * (g + LEAD - 1) + bank + 1)
                        scores(s, u, bank)
                if w == 0 and not first:
                    pe.wait_ge(out_read, s)
                    project(s - 1, 0)
                if w == 1 and not first:
                    pe.wait_ge(proj_read, 2 * s - 1)
                    project(s - 1, 1)
                pe.wait_ge(turn_read, 3 * g + 3)
                if w % (HALF // 2) == 0:
                    pe.wait_ge(values_placed, 2 * s + 1 + w // (HALF // 2))
                for k in range(BT):
                    done = weigh(w, k)
                done.then_inc(weighed, 1)

            pe.wait_ge(stacks.first_loaded, 16 * STACK_DMAS)
            for u in range(LEAD):
                for bank in range(3):
                    if u == LEAD - 1:
                        if bank == 0:
                            pe.wait_ge(probs_ready, 1)
                        turn(0, bank)
                    if u:
                        pe.wait_ge(exp_done, 3 * (u - 1) + bank + 1)
                    scores(0, u, bank)
            pe.wait_ge(zeroed, 2)
            pe.wait_ge(w_split, 1)
            for w in range(HALF):
                slot(0, w)
            with pe.Fori(1, HALVES - 1) as s:
                for w in range(HALF):
                    slot(s, w)
            for w in range(HALF):
                slot(HALVES - 1, w, last=True)
            pe.wait_ge(out_read, HALVES)
            project(HALVES - 1, 0)
            pe.wait_ge(proj_read, 2 * HALVES - 1)
            project(HALVES - 1, 1)

        @block.scalar
        def _(act):
            def exps(s, u, bank):
                act.wait_ge(shift_ready, 3 * (HALF * s + u) + bank + 1)
                for i, col in SCORE_TILES[bank]:
                    c = STAT[i]
                    last = act.activation(probs[u % 4][:, TRI[i]:TRI[i] + (i + 1) * P], score_bank[bank][:, col:col + (i + 1) * P],
                                          ACT.Exp, bias=shift[:, u % 4, c:c + 1], scale=SCALE1, accum_out=total[:, u % 4, c:c + 1])
                last.then_inc(exp_done, 1)

            def turned(s, v, group):
                g = HALF * s + v
                act.wait_ge(turn_ready, 3 * g + group + 1)
                if group == 0 and not (isinstance(g, int) and g < 2):
                    act.wait_ge(weighed, g - 1)
                at = KEY_AT[TURN_TILES[group][0]]
                width = sum((BT - k) * P for k in TURN_TILES[group])
                act.copy(pT[v % 2][0][:, at:at + width], turn_bank[group][:, 0:width]).then_inc(turn_high, 1)

            def slot(s, w, last=False):
                v, u = w + 1, w + LEAD
                turning, scoring = not (last and v >= HALF), not (last and u >= HALF)
                if turning:
                    turned(s, v, 1)
                    turned(s, v, 2)
                if scoring:
                    exps(s, u, 0)
                    exps(s, u, 1)
                if not (last and v + 1 >= HALF):
                    turned(s, v + 1, 0)
                if scoring:
                    exps(s, u, 2)
                if w == HALF - 1:
                    act.wait_ge(weighed, HALF * (s + 1))
                    act.copy(oT[0][:, :], out_bank[:, :]).then_inc(out_high, 1)

            act.wait_ge(w_loaded, 16)
            act.copy(w_pair[0][:, :, :], w_raw[:, :, :]).then_inc(w_high, 1)
            for u in range(LEAD - 1):
                for bank in range(3):
                    exps(0, u, bank)
            for bank in range(3):
                turned(0, 0, bank)
            exps(0, LEAD - 1, 0)
            exps(0, LEAD - 1, 1)
            turned(0, 1, 0)
            exps(0, LEAD - 1, 2)
            for w in range(HALF):
                slot(0, w)
            with act.Fori(1, HALVES - 1) as s:
                for w in range(HALF):
                    slot(s, w)
            for w in range(HALF):
                slot(HALVES - 1, w, last=True)

        @block.vector
        def _(dve):
            def place(s, half, count):
                heads = slice(half * HALF // 2, (half + 1) * HALF // 2)
                src = values[:, bass.ds(s, 1), :, :].rearrange("p a k (h d) -> p h (a k) d", h=HALF)[:, heads]
                high, low = (t[:, :].rearrange("p (h g) -> p h g", h=HALF)[:, heads, 0:BT * P].rearrange("p h (k c) -> p h k c", k=BT)[:, :, :, 0:DH1] for t in placed)
                dve.tensor_scalar(high, src, 1.0, None, ALU.mult).then_inc(placed_high, 1)
                dve.wait_ge(placed_high, count + 1)
                dve.tensor_tensor(low, src, f32(high), ALU.subtract).then_inc(values_placed, 1)

            def peak_of(s, u, bank):
                g = HALF * s + u
                dve.wait_ge(scores_ready, 3 * g + bank + 1)
                for i, col in SCORE_TILES[bank]:
                    c = STAT[i]
                    last = dve.reduce_max(peak[:, u % 4, c:c + 1], score_bank[bank][:, col:col + (i + 1) * P], AX.X)
                last.then_inc(peaks, 1)
                dve.wait_ge(peaks, 3 * g + bank + 1)
                lo, hi = STATS_OF_BANK[bank]
                dve.tensor_scalar(shift[:, u % 4, lo:hi], peak[:, u % 4, lo:hi], -SCALE1, None, ALU.mult).then_inc(shift_ready, 1)

            def invert(s, u):
                g = HALF * s + u
                dve.wait_ge(exp_done, 3 * g + 3)
                dve.reciprocal(inverse[:, u % 4, :], total[:, u % 4, :]).then_inc(inverse_ready, 1)

            def turned(s, v, group):
                dve.wait_ge(turn_high, 3 * (HALF * s + v) + group + 1)
                at = KEY_AT[TURN_TILES[group][0]]
                width = sum((BT - k) * P for k in TURN_TILES[group])
                dve.tensor_tensor(pT[v % 2][1][:, at:at + width], turn_bank[group][:, 0:width],
                                  f32(pT[v % 2][0][:, at:at + width]), ALU.subtract).then_inc(turn_read, 1)

            def add_projected(s, j):
                dve.wait_ge(proj_ready, 2 * s + j + 1)
                rows = x_sb[:, bass.ds(s // 2 * BT + 2 * j, 2), :].rearrange("p t d -> p (t d)")
                dve.tensor_tensor(rows, proj_bank[:, :], rows, ALU.add).then_inc(proj_read, 1)

            def slot(s, w, last=False):
                v, u = w + 1, w + LEAD
                turning, scoring = not (last and v >= HALF), not (last and u >= HALF)
                first = isinstance(s, int) and s == 0
                if not (last and u > HALF):
                    invert(s, u - 1)
                if scoring:
                    peak_of(s, u, 0)
                if turning:
                    turned(s, v, 1)
                if scoring:
                    peak_of(s, u, 1)
                    peak_of(s, u, 2)
                if turning:
                    turned(s, v, 2)
                if not (last and v + 1 >= HALF):
                    turned(s, v + 1, 0)
                if w in (0, 1) and not first:
                    add_projected(s - 1, w)
                if w == 2 and not first:
                    dve.wait_ge(weighed, HALF * s)
                    place(s, 1, 2 * s + 1)
                if w == HALF // 2 + 1 and not last:
                    dve.wait_ge(weighed, HALF * s + HALF // 2)
                    place(s + 1, 0, 2 * s + 2)
                if w == HALF - 1:
                    dve.wait_ge(out_high, s + 1)
                    dve.tensor_tensor(oT[1][:, :], out_bank[:, :], f32(oT[0][:, :]), ALU.subtract).then_inc(out_read, 1)

            for bank in range(3):
                peak_of(0, 0, bank)
            dve.wait_ge(w_high, 1)
            dve.tensor_tensor(w_pair[1][:, :, :], w_raw[:, :, :], f32(w_pair[0][:, :, :]), ALU.subtract).then_inc(w_split, 1)
            invert(0, 0)
            for u in range(1, LEAD - 1):
                for bank in range(3):
                    peak_of(0, u, bank)
                invert(0, u)
            dve.wait_ge(zeroed, 2)
            place(0, 0, 0)
            place(0, 1, 1)
            for bank in range(3):
                turned(0, 0, bank)
                peak_of(0, LEAD - 1, bank)
            turned(0, 1, 0)
            for w in range(HALF):
                slot(0, w)
            with dve.Fori(1, HALVES - 1) as s:
                for w in range(HALF):
                    slot(s, w)
            for w in range(HALF):
                slot(HALVES - 1, w, last=True)
            for j in range(2):
                add_projected(HALVES - 1, j)

E1, DF1 = 16, 176
REST1 = DF1 - P
SLOT_TILES = 2 * TILES + E1
RING1 = 4
DIGITS = RING1 + 2
assert E1 ** DIGITS <= 2 ** 24


def past(s, n):
    return not isinstance(s, int) or s >= n


def begin_zero_rows(nc, zero_row, rows_dram, rows_zeroed):
    with ExitStack() as ctx:
        m = Memory(nc, ctx, "zr")
        zero_ready = m.sem("zero_ready")
        block = ctx.enter_context(nc.Block())

        @block.gpsimd
        def _(pool):
            pool.memset(zero_row[:, :, :], 0.0).then_inc(zero_ready, 1)

        @block.sync
        def _(sp):
            sp.wait_ge(zero_ready, 1)
            sp.dma_start(rows_dram.rearrange("(s p) d -> p s d", p=P),
                         zero_row[:, :, :].to_broadcast([P, SLOT_TILES, DM])).then_inc(rows_zeroed, 16)


class ExpertLoads:

    def __init__(self, m):
        self.w13, self.w2 = m.sb("w13_lo", [P, E1, DK, 2 * DF1], F32R), m.sb("w2_lo", [P, E1, 2, DM], F32R)
        self.router = m.sb("router", [P, DK, E1])
        self.w13_loaded, self.w2_loaded, self.router_loaded = m.sem("w13_loaded"), m.sem("w2_loaded"), m.sem("router_loaded")

    def start(self, sp, gate_w, w1, w3, w2):
        sp.dma_start(self.router[:, :, :], gate_w.rearrange("(k p) e -> p k e", p=P)).then_inc(self.router_loaded, 16)
        for i, w in enumerate((w1, w3)):
            for k in range(DK):
                sp.dma_start(f32(self.w13[:, :, k, i * DF1:(i + 1) * DF1]), w[:, k * P:(k + 1) * P, :].rearrange("e p n -> p e n")).then_inc(self.w13_loaded, 16)
        sp.dma_start(f32(self.w2[:, :, 0, :]), w2[:, 0:P, :].rearrange("e p n -> p e n")).then_inc(self.w2_loaded, 16)
        sp.dma_start(f32(self.w2[0:REST1, :, 1, :]), w2[:, P:DF1, :].rearrange("e p n -> p e n")).then_inc(self.w2_loaded, 16)


def route1_phase(nc, loads, xnT, ident, slot_of, share, experts_of):
    with ExitStack() as ctx:
        m = Memory(nc, ctx, "r1")
        raw, raw_loaded = loads.router, loads.router_loaded
        router = m.pair("router", [P, DK, E1])
        before = m.sb("before", [P, P], BF16)
        ones = m.sb("ones", [P, P], BF16)
        ids = m.sb("ids", [P, E1])
        full = m.sb("full", [P, TILES])
        tile_ids = m.sb("tile_ids", [P, SLOT_TILES])
        logits_T = m.sb("logits_T", [E1, TOKENS])
        probs = m.sb("probs", [P, TILES, E1])
        stat = m.sb("stat", [P, 2, TILES])
        top = m.sb("top", [P, TILES, 8])
        top_at = m.sb("top_at", [P, TILES, 8], mybir.dt.uint32)
        top_id = m.sb("top_id", [P, TILES, 2])
        hit = m.sb("hit", [P, 2, TILES * E1])
        hits_bf = m.sb("hits_bf", [P, TILES * E1], BF16)
        square = m.sb("square", [P, E1, E1])
        order = m.sb("order", [P, E1, E1])
        tiles_of = m.sb("tiles_of", [P, E1])
        tiles_to = m.sb("tiles_to", [P, E1])
        base = m.sb("base", [P, E1])
        slots = m.sb("slots", [P, TILES, E1])
        picked = m.sb("picked", [P, 2, TILES * E1])
        slot_f = m.sb("slot_f", [P, 2, TILES])
        ended = m.sb("ended", [P, SLOT_TILES, E1])
        expert_f = m.sb("expert_f", [P, SLOT_TILES + 2 + RING1])
        packed = m.sb("packed", [P, SLOT_TILES // RING1])
        logit_bank, rank_bank, count_bank = m.ps("logit"), m.ps("rank"), m.ps("count")
        router_high, router_split = m.sem("router_high"), m.sem("router_split")
        logits_ready, shifted, exp_ready, hits_ready, counted = (m.sem(n) for n in ("logits_ready", "shifted", "exp_ready", "hits_ready", "counted"))
        logits_made, logits_copied = m.sem("logits_made"), m.sem("logits_copied")
        made_bank = [m.ps(f"made{b}") for b in range(BATCH)]
        filled, tables_ready, chain = m.sem("filled"), m.sem("tables_ready"), m.sem("chain")
        block = ctx.enter_context(nc.Block())

        @block.gpsimd
        def _(pool):
            pool.memset(ones[:, :], 1.0).then_inc(tables_ready, 1)
            pool.memset(before[:, :], 1.0).then_inc(filled, 1)
            for t, step, n in ((ids, 1, E1), (full, P, TILES), (tile_ids, 1, SLOT_TILES)):
                pool.iota(t[:, :], pattern=[[step, n]], base=0, channel_multiplier=0,
                          allow_small_or_imprecise_dtypes=True).then_inc(tables_ready, 1)
            pool.wait_ge(filled, 1)
            pool.affine_select(out=before[:, :], in_=before[:, :], compare_op=ALU.is_gt, fill=0.0, base=0,
                               pattern=[[1, P]], channel_multiplier=-1).then_inc(tables_ready, 1)

        @block.tensor
        def _(pe):
            pe.wait_ge(router_split, 1)
            for b in range(BATCH):
                for k in range(DK):
                    last = split_matmul(pe, made_bank[b][0:E1, :], both(router, slice(None), k),
                                        both(xnT, slice(None), k, slice(b * SEQ, (b + 1) * SEQ)), k == 0, k == DK - 1)
                last.then_inc(logits_made, 1)
            for t in range(TILES):
                if t % BT == 0:
                    pe.wait_ge(logits_copied, t // BT + 1)
                last = pe.transpose(logit_bank[:, t * E1:(t + 1) * E1], logits_T[:, t * P:(t + 1) * P], ident[0:E1, 0:E1])
            last.then_inc(logits_ready, 1)
            pe.wait_ge(tables_ready, 5)
            pe.wait_ge(hits_ready, 1)
            every = TILES * E1
            pe.matmul(rank_bank[:, 0:every], before[:, :], hits_bf[:, :], start=True, stop=False)
            for s in range(1, TILES):
                pe.matmul(rank_bank[:, s * E1:every], ones[:, :], hits_bf[:, 0:every - s * E1], start=False, stop=s == TILES - 1)
            for t in range(TILES):
                last = pe.matmul(count_bank[:, 0:E1], ones[:, :], hits_bf[:, t * E1:(t + 1) * E1], start=t == 0, stop=t == TILES - 1)
            last.then_inc(counted, 1)

        @block.scalar
        def _(act):
            act.wait_ge(raw_loaded, 16)
            act.copy(router[0][:, :, :], raw[:, :, :]).then_inc(router_high, 1)
            for b in range(BATCH):
                act.wait_ge(logits_made, b + 1)
                act.copy(logits_T[:, b * SEQ:(b + 1) * SEQ], made_bank[b][0:E1, :]).then_inc(logits_copied, 1)
            act.wait_ge(shifted, 1)
            act.activation(probs[:, :, :], probs[:, :, :], ACT.Exp).then_inc(exp_ready, 1)

        @block.vector
        def _(dve):
            count = [0]

            def mine(instruction):
                count[0] += 1
                instruction.then_inc(chain, 1)
                dve.wait_ge(chain, count[0])

            def down(ap, n, inner):
                return ap.rearrange("p (n a) -> p n a", a=1).to_broadcast([P, n, inner])

            def across(ap, outer, n):
                return ap.rearrange("p (a n) -> p a n", a=1).to_broadcast([P, outer, n])

            mine(dve.memset(expert_f[:, :], 0.0))
            dve.wait_ge(router_high, 1)
            dve.tensor_tensor(router[1][:, :, :], raw[:, :, :], f32(router[0][:, :, :]), ALU.subtract).then_inc(router_split, 1)
            dve.wait_ge(tables_ready, 5)
            mine(dve.tensor_tensor(order[:, :, :], down(ids[:, :], E1, E1), across(ids[:, :], E1, E1), ALU.is_ge))
            logits = logit_bank[:, 0:TILES * E1].rearrange("p (t e) -> p t e", e=E1)
            dve.wait_ge(logits_ready, 1)
            mine(dve.reduce_max(stat[:, 0, :], logits, AX.X))
            dve.tensor_tensor(probs[:, :, :], logits, down(stat[:, 0, :], TILES, E1), ALU.subtract).then_inc(shifted, 1)
            dve.wait_ge(exp_ready, 1)
            mine(dve.reduce_sum(stat[:, 1, :], probs[:, :, :], AX.X))
            mine(dve.reciprocal(stat[:, 0, :], stat[:, 1, :]))
            mine(dve.tensor_tensor(probs[:, :, :], probs[:, :, :], down(stat[:, 0, :], TILES, E1), ALU.mult))
            for t in range(TILES):
                last = dve.max(top[:, t, :], probs[:, t, :])
            mine(last)
            for t in range(TILES):
                last = dve.max_index(top_at[:, t, :], top[:, t, :], probs[:, t, :])
            mine(last)
            dve.tensor_copy(top_id[:, :, :], top_at[:, :, 0:2])
            mine(dve.tensor_tensor(stat[:, 0, :], top[:, :, 0], top[:, :, 1], ALU.add))
            mine(dve.reciprocal(stat[:, 1, :], stat[:, 0, :]))
            for j in range(2):
                dve.tensor_tensor(share[:, j, :], top[:, :, j], stat[:, 1, :], ALU.mult)
            hits = [hit[:, j, :].rearrange("p (t e) -> p t e", e=E1) for j in range(2)]
            for j in range(2):
                last = dve.tensor_tensor(hits[j], across(ids[:, :], TILES, E1), top_id[:, :, j:j + 1].to_broadcast([P, TILES, E1]), ALU.is_equal)
            mine(last)
            dve.tensor_tensor(hits_bf[:, :], hit[:, 0, :], hit[:, 1, :], ALU.add).then_inc(hits_ready, 1)
            dve.wait_ge(counted, 1)
            mine(dve.tensor_tensor(square[:, :, :], down(count_bank[:, 0:E1], E1, TILES), across(full[:, :], E1, TILES), ALU.is_gt))
            mine(dve.reduce_sum(tiles_of[:, :], square[:, :, :], AX.X))
            mine(dve.tensor_tensor(square[:, :, :], order[:, :, :], across(tiles_of[:, :], E1, E1), ALU.mult))
            mine(dve.reduce_sum(tiles_to[:, :], square[:, :, :], AX.X))
            mine(dve.tensor_tensor(base[:, :], tiles_to[:, :], tiles_of[:, :], ALU.subtract))
            mine(dve.tensor_scalar(base[:, :], base[:, :], float(P), None, ALU.mult))
            ranks = rank_bank[:, 0:TILES * E1].rearrange("p (t e) -> p t e", e=E1)
            mine(dve.tensor_tensor(slots[:, :, :], ranks, across(base[:, :], TILES, E1), ALU.add))
            for j in range(2):
                last = dve.tensor_tensor(picked[:, j, :], hit[:, j, :], slots[:, :, :].rearrange("p t e -> p (t e)"), ALU.mult)
            mine(last)
            mine(dve.reduce_sum(slot_f[:, :, :], picked[:, :, :].rearrange("p j (t e) -> p j t e", e=E1), AX.X))
            dve.tensor_copy(slot_of[:, :, :], slot_f[:, :, :])
            mine(dve.tensor_tensor(ended[:, :, :], down(tile_ids[:, :], SLOT_TILES, E1), across(tiles_to[:, :], SLOT_TILES, E1), ALU.is_ge))
            real = expert_f[:, 2:2 + SLOT_TILES]
            mine(dve.reduce_sum(real, ended[:, :, :], AX.X))
            mine(dve.tensor_scalar(real, real, float(E1 - 1), None, ALU.min))
            for i in range(DIGITS):
                digit = expert_f[:, i:i + SLOT_TILES].rearrange("p (q r) -> p q r", r=RING1)[:, :, 0]
                if i == 0:
                    mine(dve.tensor_copy(packed[:, :], digit))
                else:
                    mine(dve.scalar_tensor_tensor(packed[:, :], digit, float(E1 ** i), packed[:, :], ALU.mult, ALU.add))
            dve.tensor_copy(experts_of[:, :], packed[:, :])


def experts1_phase(nc, xn, slot_of, experts_of, rows_dram, outs_dram, rows_zeroed, w13, w2, w13_loaded, w2_loaded, ident):
    with ExitStack() as ctx:
        m = Memory(nc, ctx, "e1")
        rows = m.sb("rows", [P, RING1, DM])
        xT = [m.pair(f"xT{i}", [P, DK * P]) for i in range(2)]
        gate = m.sb("gate", [P, 2, DF1])
        h = m.sb("h", [P, 2, 2 * P])
        hT = [m.pair(f"hT{i}", [P, 2 * P]) for i in range(2)]
        outs = m.sb("outs", [P, RING1, DM])
        x_bank, up_bank, h_bank, down_bank = ([m.ps(f"{n}{i}") for i in range(2)] for n in ("x", "up", "h", "down"))
        scattered = m.sem("scattered")
        w_high, w_split, padded = m.sem("w_high"), m.sem("w_split"), m.sem("padded")
        loaded = [m.sem(f"loaded{i}") for i in range(RING1)]
        stored = [m.sem(f"stored{i}") for i in range(RING1)]
        x_turned, x_high, x_low = m.sem("x_turned"), m.sem("x_high"), m.sem("x_low")
        up_ready, gate_ready, h_ready = m.sem("up_ready"), m.sem("gate_ready"), m.sem("h_ready")
        h_turned, h_high, h_low = m.sem("h_turned"), m.sem("h_high"), m.sem("h_low")
        down_ready, out_ready = m.sem("down_ready"), m.sem("out_ready")
        block = ctx.enter_context(nc.Block())
        STEPS = SLOT_TILES // RING1
        CUT = 4

        def pieces():
            for e in range(0, E1, CUT):
                yield both(w13, slice(None), slice(e, e + CUT)), w13_loaded, 16 * 2 * DK
            for e in range(0, E1, CUT):
                yield both(w2, slice(None), slice(e, e + CUT), 0), w2_loaded, 16 * 2
                yield both(w2, slice(0, REST1), slice(e, e + CUT), 1), w2_loaded, 16 * 2

        def run(eng, tile_step):
            tile_step(0, -1)
            for q in range(2):
                for r in range(RING1):
                    tile_step(q, r)
            with eng.Fori(2, STEPS - 1) as q:
                for r in range(RING1):
                    tile_step(q, r)
            for r in range(RING1 + 2):
                tile_step(STEPS - 1, r)

        def exists(s):
            return not isinstance(s, int) or 0 <= s < SLOT_TILES

        @block.gpsimd
        def _(pool):
            for i in range(2):
                pool.memset(h[:, i, :], 0.0).then_inc(padded, 1)
            pool.wait_ge(rows_zeroed, 16)
            for t in range(TILES):
                for j in range(2):
                    pool.indirect_dma_start(rows_dram[:, :], bass.IndirectOffsetOnAxis(ap=slot_of[:, j, t:t + 1], axis=0),
                                            xn[:, t, :], None).then_inc(scattered, 16)
            pool.wait_ge(scattered, 16 * 2 * TILES)

        @block.sync
        def _(sp):
            def load(q, r):
                s = RING1 * q + r
                if past(s, RING1):
                    sp.wait_ge(x_turned, s - RING1 + 1)
                sp.dma_start(rows[:, r % RING1, :], rows_dram[bass.ds(s * P, P), :]).then_inc(loaded[r % RING1], 16)

            def tile_step(q, r):
                s = RING1 * q + r
                if exists(s + RING1) and not (isinstance(s, int) and s < 0):
                    load(q, r + RING1)
                if exists(s - 2):
                    sp.wait_ge(out_ready, s - 1)
                    sp.dma_start(outs_dram[bass.ds((s - 2) * P, P), :], outs[:, (r - 2) % RING1, :]).then_inc(stored[(r - 2) % RING1], 16)

            sp.wait_ge(scattered, 16 * 2 * TILES)
            for r in range(RING1):
                load(0, r)
            run(sp, tile_step)
            for i in range(RING1):
                sp.wait_ge(stored[i], 16 * STEPS)

        @block.tensor
        def _(pe):
            packed = [None]

            def expert_at(i):
                return packed[0] // E1 ** i % E1

            def of_expert(pair, rows_, e, k):
                return tuple(t[rows_, bass.ds(e, 1), k, :].rearrange("p a n -> p (a n)") for t in pair)

            def tile_step(q, r):
                s = RING1 * q + r
                if r == 0:
                    packed[0] = pe.value_load(experts_of[0:1, bass.ds(q, 1)], min_val=0, max_val=E1 ** DIGITS - 1)
                if exists(s + 1):
                    pe.wait_ge(loaded[(r + 1) % RING1], 16 * (q + (r + 1) // RING1 + 1))
                    if past(s + 1, 2):
                        pe.wait_ge(x_low, s)
                    for k in range(DK):
                        last = pe.transpose(x_bank[(r + 1) % 2][:, k * P:(k + 1) * P], rows[:, (r + 1) % RING1, k * P:(k + 1) * P], ident[:, :])
                    last.then_inc(x_turned, 1)
                if exists(s):
                    e = expert_at(r + 2)
                    pe.wait_ge(x_low, s + 1)
                    if past(s, 2):
                        pe.wait_ge(h_ready, s - 1)
                    for k in range(DK):
                        last = split_matmul(pe, up_bank[r % 2][:, 0:2 * DF1], both(xT[r % 2], slice(None), slice(k * P, (k + 1) * P)),
                                            of_expert(w13, slice(None), e, k), k == 0, k == DK - 1)
                    last.then_inc(up_ready, 1)
                if exists(s - 1):
                    pe.wait_ge(h_ready, s)
                    if past(s - 1, 2):
                        pe.wait_ge(h_low, s - 2)
                    for k in range(2):
                        last = pe.transpose(h_bank[(r - 1) % 2][:, k * P:(k + 1) * P], h[:, (r - 1) % 2, k * P:(k + 1) * P], ident[:, :])
                    last.then_inc(h_turned, 1)
                if exists(s - 2):
                    e = expert_at(r)
                    pe.wait_ge(h_low, s - 1)
                    if past(s - 2, 2):
                        pe.wait_ge(out_ready, s - 3)
                    for k, rows_ in enumerate((slice(0, P), slice(0, REST1))):
                        last = split_matmul(pe, down_bank[r % 2][:, 0:DM], both(hT[r % 2], rows_, slice(k * P, (k + 1) * P)),
                                            of_expert(w2, rows_, e, k), k == 0, k == 1)
                    last.then_inc(down_ready, 1)

            pe.wait_ge(w_split, len(list(pieces())))
            pe.wait_ge(padded, 2)
            run(pe, tile_step)

        @block.scalar
        def _(act):
            for (high, low), load, count in pieces():
                act.wait_ge(load, count)
                act.copy(high, f32(low)).then_inc(w_high, 1)

            def tile_step(q, r):
                s = RING1 * q + r
                if exists(s + 1):
                    act.wait_ge(x_turned, s + 2)
                    if past(s + 1, 2):
                        act.wait_ge(up_ready, s)
                    act.copy(xT[(r + 1) % 2][0][:, :], x_bank[(r + 1) % 2][:, 0:DK * P]).then_inc(x_high, 1)
                if exists(s):
                    act.wait_ge(up_ready, s + 1)
                    if past(s, 2):
                        act.wait_ge(h_ready, s - 1)
                    act.activation(gate[:, r % 2, :], up_bank[r % 2][:, 0:DF1], ACT.Silu).then_inc(gate_ready, 1)
                if exists(s - 1):
                    act.wait_ge(h_turned, s)
                    if past(s - 1, 2):
                        act.wait_ge(down_ready, s - 2)
                    act.copy(hT[(r - 1) % 2][0][:, :], h_bank[(r - 1) % 2][:, 0:2 * P]).then_inc(h_high, 1)
                if exists(s - 2):
                    act.wait_ge(down_ready, s - 1)
                    if past(s - 2, RING1):
                        act.wait_ge(stored[(r - 2) % RING1], 16 * (q + (r - 2) // RING1))
                    act.copy(outs[:, (r - 2) % RING1, :], down_bank[r % 2][:, 0:DM]).then_inc(out_ready, 1)

            run(act, tile_step)

        @block.vector
        def _(dve):
            for n, ((high, low), _, _) in enumerate(pieces()):
                dve.wait_ge(w_high, n + 1)
                dve.tensor_tensor(low, f32(low), f32(high), ALU.subtract).then_inc(w_split, 1)
            dve.wait_ge(padded, 2)

            def tile_step(q, r):
                s = RING1 * q + r
                if exists(s + 1):
                    dve.wait_ge(x_high, s + 2)
                    dve.tensor_tensor(xT[(r + 1) % 2][1][:, :], x_bank[(r + 1) % 2][:, 0:DK * P], f32(xT[(r + 1) % 2][0][:, :]),
                                      ALU.subtract).then_inc(x_low, 1)
                if exists(s):
                    dve.wait_ge(gate_ready, s + 1)
                    if past(s, 2):
                        dve.wait_ge(h_turned, s - 1)
                    dve.tensor_tensor(h[:, r % 2, 0:DF1], up_bank[r % 2][:, DF1:2 * DF1], gate[:, r % 2, :], ALU.mult).then_inc(h_ready, 1)
                if exists(s - 1):
                    dve.wait_ge(h_high, s)
                    dve.tensor_tensor(hT[(r - 1) % 2][1][:, :], h_bank[(r - 1) % 2][:, 0:2 * P], f32(hT[(r - 1) % 2][0][:, :]),
                                      ALU.subtract).then_inc(h_low, 1)

            run(dve, tile_step)


def combine1_phase(nc, x_sb, slot_of, share, outs_dram, out_dram):
    with ExitStack() as ctx:
        m = Memory(nc, ctx, "c1")
        picked = m.sb("picked", [P, 2, TILES, DM])
        gathered = [m.sem(f"gathered{b}") for b in range(BATCH)]
        first_added, added, stored = m.sem("first_added"), m.sem("added"), m.sem("stored")
        block = ctx.enter_context(nc.Block())

        @block.gpsimd
        def _(pool):
            for t in range(TILES):
                for j in range(2):
                    pool.indirect_dma_start(picked[:, j, t, :], None, outs_dram[:, :],
                                            bass.IndirectOffsetOnAxis(ap=slot_of[:, j, t:t + 1], axis=0)).then_inc(gathered[t // BT], 16)

        @block.vector
        def _(dve):
            for b in range(BATCH):
                dve.wait_ge(gathered[b], 16 * 2 * BT)
                for j in range(2):
                    if j:
                        dve.wait_ge(first_added, BT * (b + 1))
                    for t in range(b * BT, (b + 1) * BT):
                        dve.scalar_tensor_tensor(x_sb[:, t, :], picked[:, j, t, :], share[:, j, t:t + 1], x_sb[:, t, :],
                                                 ALU.mult, ALU.add).then_inc(added if j else first_added, 1)

        @block.sync
        def _(sp):
            for b in range(BATCH):
                sp.wait_ge(added, BT * (b + 1))
                sp.dma_start(out_dram[b].rearrange("(t p) d -> p t d", p=P), x_sb[:, b * BT:(b + 1) * BT, :]).then_inc(stored, 16)
            sp.wait_ge(stored, 16 * BATCH)


def two_layers(nc, x, Wq, bq, Wk, bk, Wv, bv, Wo, bo, w_router, w_fc, w_proj, w_qkv, w_out, gate_w, w1, w3, w2, out):
    with ExitStack() as ctx:
        m = Memory(nc, ctx, "all")
        x_sb = m.sb("x", [P, TILES, DM])
        ident = m.sb("ident", [P, P])
        ident_bf = m.sb("ident_bf", [P, P], BF16)
        causal_bf = m.sb("causal_bf", [P, P], BF16)
        zero_row = m.sb("zero_row", [P, 1, DM])
        slot_of = m.sb("slot_of", [P, 2, TILES], mybir.dt.uint32)
        share = m.sb("share", [P, 2, TILES])
        experts_of = m.sb("experts_of", [P, SLOT_TILES // RING1], I32)
        parts_dram = nc.dram_tensor("qk_parts", [2, 3, BATCH, DM, SEQ], BF16, kind="Internal").ap()
        rows_dram = nc.dram_tensor("slot_rows", [SLOT_TILES * P, DM], F32, kind="Internal").ap()
        outs_dram = nc.dram_tensor("slot_outs", [SLOT_TILES * P, DM], F32, kind="Internal").ap()
        rows_zeroed = m.sem("rows_zeroed")
        x_loaded = [m.sem(f"x_loaded{b}") for b in range(BATCH)]
        ln_signals = [m.sem("ln_" + name) for name in LN_SIGNALS]

        constants_phase(nc, x, x_loaded, x_sb, ident, ident_bf, causal_bf)
        with ExitStack() as layer:
            xnT = Memory(nc, layer, "l0").pair("xnT", [P, DK, TOKENS])
            with ExitStack() as part:
                loads = Attention0Loads(Memory(nc, part, "l0a"))
                layernorm_phase(nc, "ln0", ln_signals, 0, x_sb, ident, xnT, x_loaded=x_loaded,
                                loads=lambda sp: loads.start(sp, Wq, bq, Wk, bk, Wv, bv, Wo, bo))
                attention0_phase(nc, loads, x_sb, xnT, ident, ident_bf, causal_bf, Wk, Wv, Wo)
            begin_zero_rows(nc, zero_row, rows_dram, rows_zeroed)
            layernorm_phase(nc, "ln1", ln_signals, 1, x_sb, ident, xnT)
            moe0_phase(nc, x_sb, xnT, ident, w_router, w_fc, w_proj)
        with ExitStack() as layer:
            l1 = Memory(nc, layer, "l1")
            values = l1.sb("values", [P, HALVES, BT, P])
            loads, stacks = Attention1Loads(l1), Stacks(l1, parts_dram)
            with ExitStack() as part:
                xnT = Memory(nc, part, "l1").pair("xnT", [P, DK, TOKENS])
                layernorm_phase(nc, "ln2", ln_signals, 2, x_sb, ident, xnT, loads=lambda sp: loads.start(sp, w_qkv, w_out))
                project1_phase(nc, loads, stacks, xnT, parts_dram, values)
            attention1_phase(nc, loads, stacks, x_sb, values, ident, ident_bf, causal_bf)
        with ExitStack() as layer:
            l1 = Memory(nc, layer, "l1f")
            xn = l1.sb("xn", [P, TILES, DM])
            loads = ExpertLoads(l1)
            with ExitStack() as part:
                xnT = Memory(nc, part, "l1f").pair("xnT", [P, DK, TOKENS])
                layernorm_phase(nc, "ln3", ln_signals, 3, x_sb, ident, xnT, xn_all=xn, loads=lambda sp: loads.start(sp, gate_w, w1, w3, w2))
                route1_phase(nc, loads, xnT, ident, slot_of, share, experts_of)
            w13 = (l1.sb("w13_hi", [P, E1, DK, 2 * DF1], F32R), loads.w13)
            w2_pair = (l1.sb("w2_hi", [P, E1, 2, DM], F32R), loads.w2)
            experts1_phase(nc, xn, slot_of, experts_of, rows_dram, outs_dram, rows_zeroed, w13, w2_pair,
                           loads.w13_loaded, loads.w2_loaded, ident)
        combine1_phase(nc, x_sb, slot_of, share, outs_dram, out)


_INS = ["L0_attn_x", "L0_attn_Wq", "L0_attn_bq", "L0_attn_Wk", "L0_attn_bk", "L0_attn_Wv", "L0_attn_bv", "L0_attn_Wo",
        "L0_attn_bo", "L0_ffn_w_router", "L0_ffn_w_fc", "L0_ffn_w_proj", "L1_attn_w_qkv", "L1_attn_w_out",
        "L1_ffn_gate_w", "L1_ffn_w1", "L1_ffn_w3", "L1_ffn_w2"]
_OUTS = [((4, 512, 256), "float32")]


def kernel(**inputs):
    import numpy as _np
    import concourse.bacc as _bacc
    from concourse import mybir as _mybir
    from concourse.bass_utils import run_bass_kernel_spmd as _run

    nc = _bacc.Bacc("TRN2", target_bir_lowering=False, num_devices=1)
    arrays, args = {}, []
    for name in _INS:
        a = _np.ascontiguousarray(inputs[name])
        arrays[f"in_{name}_dram"] = a
        args.append(nc.dram_tensor(f"in_{name}_dram", a.shape, _mybir.dt.from_np(a.dtype), kind="ExternalInput").ap())
    for i, (shape, dtype) in enumerate(_OUTS):
        dt = _mybir.dt.from_np(_np.dtype(dtype))
        args.append(nc.dram_tensor(f"out_{i}_dram", shape, dt, kind="ExternalOutput").ap())
    two_layers(nc, *args)
    r = _run(nc, [arrays], core_ids=[0])
    got = tuple(r.results[0][f"out_{i}_dram"] for i in range(len(_OUTS)))
    return got[0]
```
